# Optimizing a Trainium2 kernel written in Bass

```python
import numpy as np
import jax
import jax.numpy as jnp

def _softmax(x, axis=-1):
    return jax.nn.softmax(x, axis=axis)

def _gelu(x):
    return jax.nn.gelu(x, approximate=True)

def _silu(x):
    return jax.nn.silu(x)

def _sigmoid(x):
    return jax.nn.sigmoid(x)

def _layernorm(x, axis=-1, eps=1e-05):
    m = jnp.mean(x, axis=axis, keepdims=True)
    v = jnp.var(x, axis=axis, keepdims=True)
    return (x - m) / jnp.sqrt(v + eps)

def _scatter_add(tgt, idx, src, axis=0):
    return tgt.at[idx].add(src)

def _segment_sum(src, seg, n):
    return jax.ops.segment_sum(src, seg, n)
kernel_name = 'mk_gnn_preln_d1_gnn_r32_ec85f5'

def setup_inputs(seed: int=0):
    np.random.seed(seed)
    _w = jnp.asarray

    def _rec_inputs():
        import jax
        import jax.numpy as jnp
        _gk = jax.random.key(seed)
        x = -0.0005121 + 1.001 * jax.random.normal(jax.random.fold_in(_gk, 1), (3125, 32), jnp.float32)
        _s = jax.random.randint(jax.random.fold_in(_gk, 2), (50000,), 0, 3125, jnp.int32)
        _d = jax.random.randint(jax.random.fold_in(_gk, 3), (50000,), 0, 3125, jnp.int32)
        _loop = jnp.arange(3125, dtype=jnp.int32)
        src = jnp.concatenate([_s, _d, _loop])
        dst = jnp.concatenate([_d, _s, _loop])
        _o = jnp.argsort(dst, stable=True)
        src = src[_o]
        dst = dst[_o]
        edge_attr_32 = -0.00010739 + 0.99994 * jax.random.normal(jax.random.fold_in(_gk, 12), (103125, 32), jnp.float32)
        return (x, src, dst, edge_attr_32)
    x, src, dst, edge_attr_32 = _rec_inputs()

    def _L0_gnn_setup():
        import jax, jax.numpy as jnp
        import numpy as np
        N_NODES = 3125
        N_EDGES = 12500
        D = 32
        EH = 128
        STEPS = 6

        def _gru_cell(x, h, wih, whh, bih, bhh):
            gi = x @ wih.T + bih
            gh = h @ whh.T + bhh
            ir, iz, inn = jnp.split(gi, 3, axis=-1)
            hr, hz, hn = jnp.split(gh, 3, axis=-1)
            r = jax.nn.sigmoid(ir + hr)
            z = jax.nn.sigmoid(iz + hz)
            n = jnp.tanh(inn + r * hn)
            return (1.0 - z) * n + z * h
        key = jax.random.key(seed)
        ks = jax.random.split(key, 12)
        s = 0.05
        return {'n_feat': jax.random.normal(ks[0], (N_NODES, D), jnp.float32), 'e_feat': jax.random.normal(ks[1], (N_EDGES, D), jnp.float32), 'src': jax.random.randint(ks[2], (N_EDGES,), 0, N_NODES, jnp.int32), 'dst': jax.random.randint(ks[3], (N_EDGES,), 0, N_NODES, jnp.int32), 'lin0_w': jax.random.normal(ks[4], (D, D), jnp.float32) * s, 'lin0_b': jnp.zeros((D,), jnp.float32), 'en1_w': jax.random.normal(ks[5], (EH, D), jnp.float32) * s, 'en1_b': jnp.zeros((EH,), jnp.float32), 'en2_w': jax.random.normal(ks[6], (D * D, EH), jnp.float32) * s, 'en2_b': jnp.zeros((D * D,), jnp.float32), 'conv_bias': jnp.zeros((D,), jnp.float32), 'gru_wih': jax.random.normal(ks[7], (3 * D, D), jnp.float32) * s, 'gru_whh': jax.random.normal(ks[8], (3 * D, D), jnp.float32) * s, 'gru_bih': jnp.zeros((3 * D,), jnp.float32), 'gru_bhh': jnp.zeros((3 * D,), jnp.float32)}
    _L0_gnn_all = _L0_gnn_setup()
    _L0_gnn_in = {k: v for k, v in _L0_gnn_all.items() if k in ('lin0_w', 'lin0_b', 'en1_w', 'en1_b', 'en2_w', 'en2_b', 'conv_bias', 'gru_wih', 'gru_whh', 'gru_bih', 'gru_bhh')}
    del _L0_gnn_all
    return {'x': x, 'src': src, 'dst': dst, 'edge_attr_32': edge_attr_32, 'L0_gnn_lin0_w': _L0_gnn_in['lin0_w'], 'L0_gnn_lin0_b': _L0_gnn_in['lin0_b'], 'L0_gnn_en1_w': _L0_gnn_in['en1_w'], 'L0_gnn_en1_b': _L0_gnn_in['en1_b'], 'L0_gnn_en2_w': _L0_gnn_in['en2_w'], 'L0_gnn_en2_b': _L0_gnn_in['en2_b'], 'L0_gnn_conv_bias': _L0_gnn_in['conv_bias'], 'L0_gnn_gru_wih': _L0_gnn_in['gru_wih'], 'L0_gnn_gru_whh': _L0_gnn_in['gru_whh'], 'L0_gnn_gru_bih': _L0_gnn_in['gru_bih'], 'L0_gnn_gru_bhh': _L0_gnn_in['gru_bhh']}

def reference(x, src, dst, edge_attr_32, L0_gnn_lin0_w, L0_gnn_lin0_b, L0_gnn_en1_w, L0_gnn_en1_b, L0_gnn_en2_w, L0_gnn_en2_b, L0_gnn_conv_bias, L0_gnn_gru_wih, L0_gnn_gru_whh, L0_gnn_gru_bih, L0_gnn_gru_bhh):
    import jax
    import jax.numpy as jnp

    def _L0_gnn_ref(n_feat, e_feat, src, dst, lin0_w, lin0_b, en1_w, en1_b, en2_w, en2_b, conv_bias, gru_wih, gru_whh, gru_bih, gru_bhh):
        import jax, jax.numpy as jnp
        import numpy as np
        N_NODES = 3125
        N_EDGES = 12500
        D = 32
        EH = 128
        STEPS = 6

        def _gru_cell(x, h, wih, whh, bih, bhh):
            gi = x @ wih.T + bih
            gh = h @ whh.T + bhh
            ir, iz, inn = jnp.split(gi, 3, axis=-1)
            hr, hz, hn = jnp.split(gh, 3, axis=-1)
            r = jax.nn.sigmoid(ir + hr)
            z = jax.nn.sigmoid(iz + hz)
            n = jnp.tanh(inn + r * hn)
            return (1.0 - z) * n + z * h
        n_nodes = n_feat.shape[0]
        out = jax.nn.relu(n_feat @ lin0_w.T + lin0_b)
        h = out
        eh = jax.nn.relu(e_feat @ en1_w.T + en1_b)
        w_e = (eh @ en2_w.T + en2_b).reshape(-1, D, D)
        for _ in range(STEPS):
            msg = jnp.einsum('ei,eio->eo', out[src], w_e)
            agg = jax.ops.segment_sum(msg, dst, num_segments=n_nodes) + conv_bias
            m = jax.nn.relu(agg)
            h = _gru_cell(m, h, gru_wih, gru_whh, gru_bih, gru_bhh)
            out = h
        return out
    h = jnp.maximum(_layernorm(x, axis=-1), 0.0)
    x = x + _L0_gnn_ref(h, edge_attr_32, src, dst, L0_gnn_lin0_w, L0_gnn_lin0_b, L0_gnn_en1_w, L0_gnn_en1_b, L0_gnn_en2_w, L0_gnn_en2_b, L0_gnn_conv_bias, L0_gnn_gru_wih, L0_gnn_gru_whh, L0_gnn_gru_bih, L0_gnn_gru_bhh)
    return x

_drawn_inputs = setup_inputs


def setup_inputs(seed=0):
    import zlib

    import numpy as np

    out = dict(_drawn_inputs(seed))
    spreads = {'L0_gnn_lin0_b': (0.0, 0.1),
     'L0_gnn_en1_b': (0.0, 0.1),
     'L0_gnn_en2_b': (0.0, 0.1),
     'L0_gnn_conv_bias': (0.0, 0.779),
     'L0_gnn_gru_bih': (0.0, 0.1),
     'L0_gnn_gru_bhh': (0.0, 0.335)}
    factors = {'L0_gnn_gru_whh': 2.763}
    for name, (base, spread) in spreads.items():
        noise = np.random.default_rng([zlib.crc32(name.encode()), seed]).standard_normal(out[name].shape)
        drawn = base * np.exp(spread * noise) if base else spread * noise
        out[name] = jnp.asarray(drawn.astype(out[name].dtype))
    for name, factor in factors.items():
        out[name] = (out[name] * factor).astype(out[name].dtype)
    return out
```

```python
from contextlib import ExitStack

import numpy as np

import concourse.bass as bass
from concourse import mybir

F32 = mybir.dt.float32
I32 = mybir.dt.int32
ALU = mybir.AluOpType
ACT = mybir.ActivationFunctionType
AX = mybir.AxisListType

P = 128
N = 3125
E = 103125
D = 32
K = 128
STEPS = 6
TILES = -(-E // P)
TB = 13
BATCHES = TILES // TB
ITERS = BATCHES // 2
SLOTS = 8
ROWS = TB * SLOTS
HALF = (6, 7)
TC = SLOTS * D
CH = 25
NP = N // CH
GROUP = 4
GROUPS = -(-CH // GROUP)
ZERO = BATCHES * ROWS
G_UNITS = -(-TB // 2)
EH_GROUPS = ((0, 4), (4, 7), (7, 10), (10, 13))
LN_EPS = 1e-5
assert BATCHES * TB == TILES and ITERS * 2 == BATCHES and sum(HALF) == TB and NP * CH == N


def group_chunks(g):
    return range(g * GROUP, min(CH, g * GROUP + GROUP))


def build(nc, x, src_t, dst_t, next_t, ends, attr_t, w1, w2, b2, w_gru, w_lin, conv_b, out):
    with ExitStack() as ctx:
        def sb(name, shape, dt=F32):
            return ctx.enter_context(nc.sbuf_tensor(name, shape, dt))

        def bank(name):
            return ctx.enter_context(nc.psum_tensor(name, [P, 512], F32))

        def sem(name):
            return ctx.enter_context(nc.semaphore(name))

        table = nc.dram_tensor("node_table", (N + 1, D), F32, kind="Internal").ap()
        slot_rows = nc.dram_tensor("slot_rows", (ZERO + 2, D), F32, kind="Internal").ap()

        w1_sb = sb("w1_sb", [D + 1, K])
        w2_sb = sb("w2_sb", [K, D, D])
        b2_sb = sb("b2_sb", [D, D])
        w_gru_sb = sb("w_gru_sb", [2 * D + 2, 4 * D])
        w_lin_sb = sb("w_lin_sb", [2 * D + 2, D])
        conv_row = sb("conv_row", [1, D])
        conv_sb = sb("conv_sb", [P, D])
        ident = sb("ident", [P, P])
        ones_row = sb("ones_row", [1, P])
        zeros = sb("zeros", [2, D])
        eps = sb("eps", [P, 1])
        src_sb = sb("src_sb", [P, TILES], I32)
        mask = sb("mask", [P, TILES * SLOTS])
        idx_a = sb("idx_a", [NP, CH], I32)
        idx_b = sb("idx_b", [NP, CH], I32)
        x_sb = sb("x_sb", [NP, CH, D])
        mh = sb("mh", [NP, CH, 2 * D])
        mh_t = sb("mh_t", [2 * D + 2, CH * NP])
        agg_a = sb("agg_a", [NP, CH * D])
        agg_b = sb("agg_b", [NP, CH * D])
        gates = sb("gates", [NP, CH, 2 * D])
        cand = sb("cand", [NP, CH, D])
        cand2 = sb("cand2", [NP, CH, D])
        idx_now = [sb(f"idx_now{u}", [P, TB], I32) for u in range(2)]
        xg = [sb(f"xg{u}", [P, TB * D]) for u in range(2)]
        mask_now = [sb(f"mask_now{u}", [P, TB, SLOTS]) for u in range(2)]
        xm = [sb(f"xm{u}", [P, TB, D, SLOTS]) for u in range(2)]
        attr = [sb(f"attr{u}", [D + 1, TB * P]) for u in range(2)]
        eh = [sb(f"eh{u}", [P, TB * K]) for u in range(2)]
        g_sb = [sb(f"g_sb{u}", [K, D, TB, SLOTS]) for u in range(2)]
        xs_t = [sb(f"xs_t{u}", [D, ROWS]) for u in range(2)]
        slot_sb = [sb(f"slot_sb{u}", [ROWS, D]) for u in range(2)]

        eh_ps = [bank(f"eh_ps{i}") for i in range(2)]
        g_ps = [bank(f"g_ps{i}") for i in range(4)]
        xs_ps = bank("xs_ps")
        slot_ps = bank("slot_ps")

        x_in = sem("x_in")
        edges_in = sem("edges_in")
        src_in = sem("src_in")
        weights_in = sem("weights_in")
        zero_rows = sem("zero_rows")
        consts = sem("consts")
        consts_dve = sem("consts_dve")
        dve_order = sem("dve_order")
        ends_ps = sem("ends_ps")
        std_ready = sem("std_ready")
        mask_ready = sem("mask_ready")
        node_idx = sem("node_idx")
        idx_staged = sem("idx_staged")
        gathered = [[sem(f"gathered{u}{h}") for h in range(2)] for u in range(2)]
        mask_staged = sem("mask_staged")
        xm_ready = sem("xm_ready")
        attr_in = [sem(f"attr_in{u}") for u in range(2)]
        eh_made = sem("eh_made")
        eh_ready = sem("eh_ready")
        g_made = sem("g_made")
        xs_made = sem("xs_made")
        g_act = sem("g_act")
        g_dve = sem("g_dve")
        xs_ready = sem("xs_ready")
        slot_made = sem("slot_made")
        slot_copied = sem("slot_copied")
        slot_out = [sem(f"slot_out{u}") for u in range(2)]
        agg_in = [sem(f"agg_in{g}") for g in range(GROUPS)]
        m_ready = sem("m_ready")
        mh_made = sem("mh_made")
        mht_ready = sem("mht_ready")
        gates_made = sem("gates_made")
        rz_ready = sem("rz_ready")
        pre_ready = sem("pre_ready")
        n_ready = sem("n_ready")
        h_ready = sem("h_ready")
        table_out = sem("table_out")
        y_ready = sem("y_ready")
        out_done = sem("out_done")
        pool_passed = sem("pool_passed")
        pe_passed = sem("pe_passed")

        pre0 = g_sb[0][:, :, :, :].rearrange("p i t r -> p (i t r)")
        pre1 = g_sb[1][:, :, :, :].rearrange("p i t r -> p (i t r)")
        dst_f = pre0[:, 0:TILES]
        nxt_f = pre0[:, TILES:2 * TILES]
        first_b = pre0[:, 2 * TILES:3 * TILES]
        last_b = pre1[:, 0:TILES]
        tile_id = pre1[:, TILES:2 * TILES]
        junk = pre1[:, 2 * TILES:3 * TILES]
        dst_i = sb("dst_i", [P, TILES], I32)
        nxt_i = sb("nxt_i", [P, TILES], I32)
        ends_i = sb("ends_i", [1, 2 * TILES], I32)
        ends_f = sb("ends_f", [1, 2 * TILES])
        tid_i = sb("tid_i", [P, TILES], I32)
        node_i = sb("node_i", [NP, CH], I32)
        node_f = sb("node_f", [NP, CH])
        tile_a = sb("tile_a", [NP, CH])
        tile_b = sb("tile_b", [NP, CH])
        first_a = sb("first_a", [NP, CH])
        t0 = sb("t0", [NP, CH])
        t1 = sb("t1", [NP, CH])
        stat = sb("stat", [NP, CH])
        stat2 = sb("stat2", [NP, CH])

        block = ctx.enter_context(nc.Block())

        @block.sync
        def _(sp):
            sp.dma_start(x_sb[:, :, :], x.rearrange("(p c) d -> p c d", c=CH)).then_inc(x_in, 16)
            sp.dma_start(src_sb[:, :], src_t).then_inc(src_in, 16)
            sp.dma_start(w_lin_sb[:, :], w_lin).then_inc(weights_in, 16)
            sp.dma_start(w1_sb[:, :], w1).then_inc(weights_in, 16)
            sp.dma_start(w2_sb[:, :, :], w2).then_inc(weights_in, 16)
            sp.dma_start(b2_sb[:, :], b2).then_inc(weights_in, 16)
            sp.dma_start(w_gru_sb[:, :], w_gru).then_inc(weights_in, 16)
            sp.dma_start(conv_row[:, :], conv_b).then_inc(weights_in, 16)
            sp.dma_start(ends_i[:, :], ends).then_inc(edges_in, 16)
            sp.dma_start(dst_i[:, :], dst_t).then_inc(edges_in, 16)
            sp.dma_start(nxt_i[:, :], next_t).then_inc(edges_in, 16)
            sp.dma_start(attr[0][:, :], attr_t[:, 0:TB * P]).then_inc(attr_in[0], 16)
            sp.wait_ge(consts, 1)
            sp.dma_start(table[N:N + 1, :], zeros[0:1, :]).then_inc(table_out, 16)
            sp.wait_ge(h_ready, GROUPS)
            sp.dma_start(table[0:N, :].rearrange("(p c) d -> p c d", c=CH), mh[:, :, D:2 * D]).then_inc(table_out, 16)
            with sp.Fori(0, STEPS) as s:
                with sp.Fori(0, ITERS) as j:
                    for u in range(2):
                        n = s * BATCHES + j * 2 + u
                        sp.wait_ge(eh_made, n * 4 + 4)
                        sp.dma_start(attr[1 - u][:, :], attr_t[:, bass.ds((j * 2 + u + 1) * (TB * P), TB * P)])\
                          .then_inc(attr_in[1 - u], 16)
                sp.wait_ge(h_ready, (s + 2) * GROUPS)
                sp.dma_start(table[0:N, :].rearrange("(p c) d -> p c d", c=CH), mh[:, :, D:2 * D])\
                  .then_inc(table_out, 16)
            sp.wait_ge(y_ready, 1)
            sp.dma_start(out.rearrange("(p c) d -> p c d", c=CH), mh[:, :, 0:D]).then_inc(out_done, 16)
            sp.wait_ge(out_done, 16)
            sp.wait_ge(table_out, 16 * (STEPS + 2))
            sp.wait_ge(attr_in[0], 16 * (STEPS * ITERS + 1))
            sp.wait_ge(attr_in[1], 16 * STEPS * ITERS)

        @block.gpsimd
        def _(pool):
            pool.memset(zeros[:, :], 0.0).then_inc(consts, 1)
            pool.memset(ident[:, :], 0.0).then_inc(consts, 1)
            pool.wait_ge(consts, 2)
            pool.affine_select(out=ident[:, :], in_=ident[:, :], compare_op=ALU.not_equal, fill=1.0, base=0,
                               pattern=[[-1, P]], channel_multiplier=1).then_inc(consts, 1)
            pool.iota(node_i[:, :], pattern=[[1, CH]], base=0, channel_multiplier=CH).then_inc(consts, 1)
            pool.iota(tid_i[:, :], pattern=[[1, TILES]], base=0, channel_multiplier=0).then_inc(consts, 1)
            pool.wait_ge(src_in, 16)
            pool.wait_ge(node_idx, 1)
            with pool.Fori(0, STEPS) as s:
                pool.wait_ge(table_out, s * 16 + 32)
                pool.sem_inc(pool_passed, 1)
                with pool.Fori(0, ITERS) as j:
                    for u in range(2):
                        n = s * BATCHES + j * 2 + u
                        pool.wait_ge(xs_made, n + 1)
                        pool.tensor_copy(idx_now[u][:, :], src_sb[:, bass.ds((j * 2 + u) * TB, TB)])\
                            .then_inc(idx_staged, 1)
                        pool.wait_ge(idx_staged, n + 1)
                        pool.sem_inc(pool_passed, 1)
                        for t in range(TB):
                            pool.indirect_dma_start(
                                xg[u][:, t * D:(t + 1) * D], None, table,
                                bass.IndirectOffsetOnAxis(ap=idx_now[u][:, t:t + 1], axis=0))\
                                .then_inc(gathered[u][int(t >= HALF[0])], 16)
                for u in range(2):
                    pool.wait_ge(slot_out[u], (s + 1) * (16 * ITERS) + 16)
                    pool.sem_inc(pool_passed, 1)
                for g in range(GROUPS):
                    for c in group_chunks(g):
                        for agg, idx in ((agg_a, idx_a), (agg_b, idx_b)):
                            pool.indirect_dma_start(
                                agg[:, c * D:(c + 1) * D], None, slot_rows,
                                bass.IndirectOffsetOnAxis(ap=idx[:, c:c + 1], axis=0)).then_inc(agg_in[g], 16)

        @block.scalar
        def _(act):
            act.sem_inc(slot_copied, 1)
            act.wait_ge(consts, 1)
            for u in range(2):
                act.dma_start(slot_rows[ZERO + u:ZERO + u + 1, :], zeros[u:u + 1, :]).then_inc(slot_out[u], 16)

            act.wait_ge(std_ready, 1)
            nc.scalar.activation(stat[:, :], stat2[:, :], ACT.Sqrt, bias=eps[0:NP, :], scale=1.0 / D)\
                .then_inc(std_ready, 1)

            def transposed(g, done):
                act.wait_ge(mh_made, done + g + 1)
                w = len(group_chunks(g)) * NP
                nc.scalar.copy(mh_t[0:2 * D, g * GROUP * NP:g * GROUP * NP + w], g_ps[g % 2][0:2 * D, 0:w])\
                    .then_inc(mht_ready, 1)

            for g in range(GROUPS):
                transposed(g, 0)
                act.wait_ge(gates_made, g + 1)
                k = len(group_chunks(g))
                nc.scalar.activation(mh[:, g * GROUP:g * GROUP + k, D:2 * D],
                                     g_ps[2 + g % 2][0:NP, :].rearrange("p (c f) -> p c f", f=4 * D)[:, 0:k, 0:D],
                                     ACT.Relu).then_inc(h_ready, 1)

            def relu(n, v):
                for g, (a, b) in enumerate(EH_GROUPS):
                    act.wait_ge(eh_made, n * 4 + (4 + g + 1))
                    nc.scalar.activation(eh[v][:, a * K:b * K], eh_ps[g % 2][:, 0:(b - a) * K], ACT.Relu)\
                        .then_inc(eh_ready, 1)

            relu(0, 0)
            with act.Fori(0, STEPS) as s:
                with act.Fori(0, ITERS) as j:
                    for u in range(2):
                        n = s * BATCHES + j * 2 + u
                        for q in range(0, G_UNITS, 2):
                            act.wait_ge(g_made, n * G_UNITS + (q + 1))
                            g_copy(nc.scalar.copy, g_sb[u], g_ps, q).then_inc(g_act, 1)
                        relu(n + 1, 1 - u)
                        act.wait_ge(slot_made, n + 1)
                        act.wait_ge(slot_out[u], (s * ITERS + j) * 16 + 16)
                        nc.scalar.copy(slot_sb[u][:, :], slot_ps[0:ROWS, 0:D]).then_inc(slot_copied, 1)
                        act.wait_ge(slot_copied, n + 2)
                        act.dma_start(slot_rows[bass.ds((j * 2 + u) * ROWS, ROWS), :], slot_sb[u][:, :])\
                           .then_inc(slot_out[u], 16)
                for g in range(GROUPS):
                    k = len(group_chunks(g))
                    cs = slice(g * GROUP, g * GROUP + k)
                    transposed(g, (s + 1) * GROUPS)
                    act.wait_ge(gates_made, (s + 1) * GROUPS + (g + 1))
                    gp = g_ps[2 + g % 2][0:NP, :].rearrange("p (c f) -> p c f", f=4 * D)
                    nc.scalar.activation(gates[:, cs, :], gp[:, 0:k, 0:2 * D], ACT.Sigmoid).then_inc(rz_ready, 1)
                    act.wait_ge(pre_ready, s * GROUPS + (g + 1))
                    nc.scalar.activation(cand2[:, cs, :], cand[:, cs, :], ACT.Tanh).then_inc(n_ready, 1)
            for u in range(2):
                act.wait_ge(slot_out[u], 16 * (STEPS * ITERS + 1))

        @block.vector
        def _(dve):
            order = [0]

            def link(ins, base=0):
                order[0] += 1
                ins.then_inc(dve_order, 1)
                dve.wait_ge(dve_order, base + order[0])

            nc.vector.memset(ones_row[:, :], 1.0).then_inc(consts_dve, 1)
            nc.vector.memset(eps[:, :], LN_EPS).then_inc(consts_dve, 1)
            nc.vector.memset(mh_t[2 * D:2 * D + 2, :], 1.0).then_inc(consts_dve, 1)
            link(nc.vector.memset(mh[:, :, :], 0.0))

            def over_d(a):
                return a[:, :].unsqueeze(2).broadcast_to([NP, CH, D])

            dve.wait_ge(x_in, 16)
            link(nc.vector.reduce_sum(t0[:, :], x_sb[:, :, :], AX.X))
            link(nc.vector.tensor_scalar(t0[:, :], t0[:, :], 1.0 / D, None, ALU.mult))
            link(nc.vector.tensor_tensor(cand[:, :, :], x_sb[:, :, :], over_d(t0), ALU.subtract))
            link(nc.vector.tensor_tensor(cand2[:, :, :], cand[:, :, :], cand[:, :, :], ALU.mult))
            nc.vector.reduce_sum(stat2[:, :], cand2[:, :, :], AX.X).then_inc(std_ready, 1)
            dve.wait_ge(std_ready, 2)
            link(nc.vector.reciprocal(t1[:, :], stat[:, :]))
            link(nc.vector.tensor_tensor(cand2[:, :, :], cand[:, :, :], over_d(t1), ALU.mult))
            nc.vector.tensor_scalar_max(mh[:, :, 0:D], cand2[:, :, :], 0.0).then_inc(m_ready, GROUPS)

            dve.wait_ge(edges_in, 48)
            link(nc.vector.tensor_copy(ends_f[:, :], ends_i[:, :]))
            nc.vector.tensor_copy(dst_f, dst_i[:, :])
            nc.vector.tensor_copy(nxt_f, nxt_i[:, :])
            dve.wait_ge(ends_ps, 1)
            nc.vector.tensor_copy(first_b[:, 0:TILES // 2], g_ps[0][:, 0:TILES // 2])
            nc.vector.tensor_copy(first_b[:, TILES // 2:TILES], g_ps[1][:, 0:TILES // 2])
            nc.vector.tensor_copy(last_b[:, 0:TILES // 2], g_ps[2][:, 0:TILES // 2])
            nc.vector.tensor_copy(last_b[:, TILES // 2:TILES], g_ps[3][:, 0:TILES // 2])
            link(nc.vector.tensor_copy(conv_sb[:, :], xs_ps[:, 0:D]))
            link(nc.vector.tensor_tensor(dst_f, dst_f, first_b, ALU.subtract))
            mask_tr = mask[:, :].rearrange("p (t r) -> p t r", r=SLOTS)
            for r in range(SLOTS):
                nc.vector.tensor_single_scalar(mask_tr[:, :, r], dst_f, float(r), ALU.is_equal)\
                    .then_inc(mask_ready, 1)
            dve.wait_ge(mask_ready, SLOTS)

            dve.wait_ge(consts, 5)
            nc.vector.tensor_copy(tile_id, tid_i[:, :])
            link(nc.vector.tensor_copy(node_f[:, :], node_i[:, :]))
            for c in range(CH):
                node = node_f[:, c:c + 1]
                link(nc.vector.tensor_scalar(junk[0:NP, :], last_b[0:NP, :], node, 0.0, ALU.is_lt, ALU.add,
                                             accum_out=tile_a[:, c:c + 1]))
                link(nc.vector.tensor_scalar(junk[0:NP, :], first_b[0:NP, :], node, 0.0, ALU.is_le, ALU.add,
                                             accum_out=tile_b[:, c:c + 1]))
                link(nc.vector.scalar_tensor_tensor(junk[0:NP, :], tile_id[0:NP, :], tile_a[:, c:c + 1],
                                                    first_b[0:NP, :], ALU.is_equal, ALU.mult,
                                                    accum_out=first_a[:, c:c + 1]))
            link(nc.vector.tensor_scalar(tile_b[:, :], tile_b[:, :], -1.0, None, ALU.add))
            link(nc.vector.tensor_tensor(t0[:, :], tile_b[:, :], tile_a[:, :], ALU.subtract))
            link(nc.vector.tensor_tensor(t1[:, :], node_f[:, :], first_a[:, :], ALU.subtract))
            link(nc.vector.scalar_tensor_tensor(t1[:, :], tile_a[:, :], float(SLOTS), t1[:, :], ALU.mult, ALU.add))
            link(nc.vector.tensor_scalar(t1[:, :], t1[:, :], float(-ZERO), None, ALU.add))
            link(nc.vector.scalar_tensor_tensor(t1[:, :], t0[:, :], 0.0, t1[:, :], ALU.is_ge, ALU.mult))
            link(nc.vector.tensor_scalar(t1[:, :], t1[:, :], float(ZERO), 0.0, ALU.add, ALU.max))
            link(nc.vector.tensor_scalar(t1[:, :], t1[:, :], float(ZERO), None, ALU.min))
            link(nc.vector.tensor_copy(idx_a[:, :], t1[:, :]))
            link(nc.vector.tensor_scalar(t1[:, :], tile_b[:, :], float(SLOTS), float(-ZERO), ALU.mult, ALU.add))
            link(nc.vector.scalar_tensor_tensor(t1[:, :], t0[:, :], 1.0, t1[:, :], ALU.is_equal, ALU.mult))
            link(nc.vector.tensor_scalar(t1[:, :], t1[:, :], float(ZERO), None, ALU.add))
            nc.vector.tensor_copy(idx_b[:, :], t1[:, :]).then_inc(node_idx, 1)

            before = order[0]
            per_step = 5 * GROUPS
            with dve.Fori(0, STEPS) as s:
                with dve.Fori(0, ITERS) as j:
                    for u in range(2):
                        n = s * BATCHES + j * 2 + u
                        dve.wait_ge(xs_made, n + 1)
                        nc.vector.tensor_copy(mask_now[u][:, :, :].rearrange("p t r -> p (t r)"),
                                              mask[:, bass.ds((j * 2 + u) * ROWS, ROWS)]).then_inc(mask_staged, 1)
                        dve.wait_ge(mask_staged, n + 1)
                        t = 0
                        for h in range(2):
                            k = HALF[h]
                            dve.wait_ge(gathered[u][h], (s * ITERS + j) * (16 * k) + 16 * k)
                            xv = xg[u][:, t * D:(t + k) * D].rearrange("p (t i) -> p t i", i=D)
                            nc.vector.tensor_tensor(
                                xm[u][:, t:t + k, :, :], xv.unsqueeze(3).broadcast_to([P, k, D, SLOTS]),
                                mask_now[u][:, t:t + k, :].unsqueeze(2).broadcast_to([P, k, D, SLOTS]),
                                ALU.mult).then_inc(xm_ready, 1)
                            t += k
                        for q in range(1, G_UNITS, 2):
                            dve.wait_ge(g_made, n * G_UNITS + (q + 1))
                            g_copy(nc.vector.tensor_copy, g_sb[u], g_ps, q).then_inc(g_dve, 1)
                        dve.wait_ge(xs_made, n + 3)
                        nc.vector.tensor_copy(xs_t[u][:, :], xs_ps[0:D, 0:ROWS]).then_inc(xs_ready, 1)
                base = s * per_step
                for g in range(GROUPS):
                    k = len(group_chunks(g))
                    cs = slice(g * GROUP, g * GROUP + k)
                    fs = slice(g * GROUP * D, (g * GROUP + k) * D)
                    dve.wait_ge(agg_in[g], s * (32 * k) + 32 * k)
                    link(nc.vector.tensor_tensor(agg_a[:, fs], agg_a[:, fs], agg_b[:, fs], ALU.add), base)
                    a3 = agg_a[:, fs].rearrange("p (c d) -> p c d", d=D)
                    link(nc.vector.tensor_tensor(a3, a3, conv_sb[0:NP, :].unsqueeze(1).broadcast_to([NP, k, D]),
                                                 ALU.add), base)
                    nc.vector.tensor_scalar_max(mh[:, cs, 0:D], a3, 0.0).then_inc(m_ready, 1)
                    dve.wait_ge(rz_ready, s * GROUPS + (g + 1))
                    gp = g_ps[2 + g % 2][0:NP, :].rearrange("p (c f) -> p c f", f=4 * D)
                    link(nc.vector.tensor_tensor(cand[:, cs, :], gates[:, cs, 0:D], gp[:, 0:k, 3 * D:4 * D],
                                                 ALU.mult), base)
                    nc.vector.tensor_tensor(cand[:, cs, :], cand[:, cs, :], gp[:, 0:k, 2 * D:3 * D],
                                            ALU.add).then_inc(pre_ready, 1)
                    dve.wait_ge(n_ready, s * GROUPS + (g + 1))
                    link(nc.vector.tensor_tensor(cand[:, cs, :], mh[:, cs, D:2 * D], cand2[:, cs, :],
                                                 ALU.subtract), base)
                    link(nc.vector.tensor_tensor(cand[:, cs, :], cand[:, cs, :], gates[:, cs, D:2 * D],
                                                 ALU.mult), base)
                    nc.vector.tensor_tensor(mh[:, cs, D:2 * D], cand[:, cs, :], cand2[:, cs, :],
                                            ALU.add).then_inc(h_ready, 1)
                assert order[0] == before + per_step
            dve.wait_ge(h_ready, (STEPS + 1) * GROUPS)
            nc.vector.tensor_tensor(mh[:, :, 0:D], x_sb[:, :, :], mh[:, :, D:2 * D], ALU.add).then_inc(y_ready, 1)

        @block.tensor
        def _(pe):
            pe.sem_inc(xs_made, 2)
            pe.sem_inc(eh_made, 4)

            def node_products(g, done, w_sb, m_done):
                pe.wait_ge(m_ready, m_done)
                pe.sem_inc(pe_passed, 1)
                for i, c in enumerate(group_chunks(g)):
                    last = nc.tensor.transpose(g_ps[g % 2][0:2 * D, i * NP:(i + 1) * NP], mh[:, c, :],
                                               ident[0:NP, 0:NP])
                last.then_inc(mh_made, 1)
                pe.wait_ge(mht_ready, done + g + 1)
                for i, c in enumerate(group_chunks(g)):
                    last = nc.tensor.matmul(g_ps[2 + g % 2][0:NP, i * 4 * D:i * 4 * D + w_sb.shape[1]],
                                            mh_t[:, c * NP:(c + 1) * NP], w_sb[:, :], start=True, stop=True)
                last.then_inc(gates_made, 1)

            pe.wait_ge(consts, 3)
            pe.wait_ge(consts_dve, 3)
            pe.wait_ge(weights_in, 96)
            for g in range(GROUPS):
                if g >= 2:
                    pe.wait_ge(h_ready, g - 1)
                node_products(g, 0, w_lin_sb, GROUPS)

            pe.wait_ge(h_ready, GROUPS)
            pe.wait_ge(dve_order, 8 + 0)
            for i in range(4):
                nc.tensor.matmul(g_ps[i][:, 0:TILES // 2], ones_row[:, :],
                                 ends_f[:, i * (TILES // 2):(i + 1) * (TILES // 2)], start=True, stop=True)
            nc.tensor.matmul(xs_ps[:, 0:D], ones_row[:, :], conv_row[:, :], start=True, stop=True)\
                .then_inc(ends_ps, 1)

            def edge_network(n, v, uses):
                pe.wait_ge(attr_in[v], uses)
                for g, (a, b) in enumerate(EH_GROUPS):
                    if g >= 2:
                        pe.wait_ge(eh_ready, n * 4 + (g - 1))
                    for t in range(a, b):
                        last = nc.tensor.matmul(eh_ps[g % 2][:, (t - a) * K:(t - a + 1) * K],
                                                attr[v][:, t * P:(t + 1) * P], w1_sb[:, :], start=True, stop=True)
                    last.then_inc(eh_made, 1)

            edge_network(0, 0, 16)
            with pe.Fori(0, STEPS) as s:
                with pe.Fori(0, ITERS) as j:
                    for u in range(2):
                        n = s * BATCHES + j * 2 + u
                        pe.wait_ge(eh_ready, n * 4 + 4)
                        for q in range(G_UNITS):
                            if 2 * q in (0, HALF[0]):
                                pe.wait_ge(xm_ready, n * 2 + (1 if q == 0 else 2))
                            if q >= 4:
                                if q % 2:
                                    pe.wait_ge(g_dve, n * 3 + (q - 4 + 1) // 2)
                                else:
                                    pe.wait_ge(g_act, n * 4 + ((q - 4) // 2 + 1))
                            for t in range(2 * q, min(2 * q + 2, TB)):
                                last = nc.tensor.matmul(
                                    g_ps[q % 4][:, (t % 2) * TC:(t % 2 + 1) * TC], eh[u][:, t * K:(t + 1) * K],
                                    xm[u][:, t, :, :].rearrange("p i r -> p (i r)"), start=True, stop=True)
                            last.then_inc(g_made, 1)
                        for t in range(TB):
                            last = nc.tensor.matmul(xs_ps[0:D, t * SLOTS:(t + 1) * SLOTS],
                                                    xg[u][:, t * D:(t + 1) * D], mask_now[u][:, t, :],
                                                    start=True, stop=True)
                        last.then_inc(xs_made, 1)
                        edge_network(n + 1, 1 - u, (s * ITERS + j) * 16 + 16 * (u + 1))
                        pe.wait_ge(g_act, n * 4 + 4)
                        pe.wait_ge(g_dve, n * 3 + 3)
                        pe.wait_ge(xs_ready, n + 1)
                        pe.wait_ge(slot_copied, n + 1)
                        for i in range(D):
                            nc.tensor.matmul(slot_ps[0:ROWS, 0:D],
                                             g_sb[u][:, i, :, :].rearrange("k t r -> k (t r)"), w2_sb[:, i, :],
                                             start=(i == 0), stop=False)
                        nc.tensor.matmul(slot_ps[0:ROWS, 0:D], xs_t[u][:, :], b2_sb[:, :],
                                         start=False, stop=True).then_inc(slot_made, 1)
                for g in range(GROUPS):
                    if g >= 2:
                        pe.wait_ge(pre_ready, s * GROUPS + (g - 1))
                    node_products(g, (s + 1) * GROUPS, w_gru_sb, (s + 1) * GROUPS + (g + 1))


def g_copy(copy, g_sb, g_ps, q):
    k = min(2, TB - 2 * q)
    return copy(g_sb[:, :, 2 * q:2 * q + k, :],
                g_ps[q % 4][:, 0:k * TC].rearrange("k (t i r) -> k i t r", i=D, r=SLOTS))


def kernel(x, src, dst, edge_attr_32, L0_gnn_lin0_w, L0_gnn_lin0_b, L0_gnn_en1_w, L0_gnn_en1_b, L0_gnn_en2_w,
           L0_gnn_en2_b, L0_gnn_conv_bias, L0_gnn_gru_wih, L0_gnn_gru_whh, L0_gnn_gru_bih, L0_gnn_gru_bhh):
    import concourse.bacc as bacc
    from concourse.bass_utils import run_bass_kernel_spmd

    pad = TILES * P - E
    x, src, dst, attr, w_lin, b_lin, w1, b1, w2, b2, conv_b, wih, whh, bih, bhh = (
        np.asarray(a) for a in (x, src, dst, edge_attr_32, L0_gnn_lin0_w, L0_gnn_lin0_b, L0_gnn_en1_w, L0_gnn_en1_b,
                                L0_gnn_en2_w, L0_gnn_en2_b, L0_gnn_conv_bias, L0_gnn_gru_wih, L0_gnn_gru_whh,
                                L0_gnn_gru_bih, L0_gnn_gru_bhh))

    def zeros(*shape):
        return np.zeros(shape, np.float32)

    src_p = np.concatenate([src, np.full(pad, N, np.int32)])
    dst_p = np.concatenate([dst, np.repeat(dst[-1:], pad)])
    next_p = np.concatenate([dst_p[1:], dst_p[-1:]])
    ends = np.concatenate([dst_p[0::P], dst_p[P - 1::P]])[None, :]
    attr_t = np.concatenate([attr.T, zeros(D, pad)], 1)
    attr_t = np.concatenate([attr_t, np.ones((1, TILES * P), np.float32)], 0)
    attr_t = np.concatenate([attr_t, attr_t[:, 0:TB * P]], 1)
    w_gru = np.concatenate([
        np.concatenate([wih.T, zeros(D, D)], 1),
        np.concatenate([whh.T[:, 0:2 * D], zeros(D, D), whh.T[:, 2 * D:3 * D]], 1),
        np.concatenate([bih, zeros(D)])[None, :],
        np.concatenate([bhh[0:2 * D], zeros(D), bhh[2 * D:3 * D]])[None, :]], 0)
    w_lin_t = np.concatenate([w_lin.T, zeros(D, D), b_lin[None, :], zeros(1, D)], 0)
    arrays = {
        "x_in": x,
        "src_t": src_p.reshape(TILES, P).T,
        "dst_t": dst_p.reshape(TILES, P).T,
        "next_t": next_p.reshape(TILES, P).T,
        "ends": ends,
        "attr_t": attr_t,
        "w1_t": np.concatenate([w1.T, b1[None, :]], 0),
        "w2_t": w2.reshape(D, D, K).transpose(2, 0, 1),
        "b2_t": b2.reshape(D, D),
        "w_gru_t": w_gru,
        "w_lin_t": w_lin_t,
        "conv_b": conv_b[None, :],
    }
    arrays = {k: np.ascontiguousarray(v) for k, v in arrays.items()}
    nc = bacc.Bacc("TRN2", target_bir_lowering=False, num_devices=1)
    args = [nc.dram_tensor(k, v.shape, mybir.dt.from_np(v.dtype), kind="ExternalInput").ap()
            for k, v in arrays.items()]
    out = nc.dram_tensor("out", (N, D), F32, kind="ExternalOutput").ap()
    build(nc, *args, out)
    r = run_bass_kernel_spmd(nc, [arrays], core_ids=[0])
    return r.results[0]["out"]
```

```python
from contextlib import ExitStack

import numpy as np

import concourse.bass as bass
from concourse import mybir

F32 = mybir.dt.float32
I32 = mybir.dt.int32
ALU = mybir.AluOpType
ACT = mybir.ActivationFunctionType
AX = mybir.AxisListType

P = 128
N = 3125
E = 103125
D = 32
K = 128
STEPS = 6
TILES = -(-E // P)
TB = 13
BATCHES = TILES // TB
ITERS = BATCHES // 2
SLOTS = 8
ROWS = TB * SLOTS
ROWS2 = 2 * ROWS
HALF = (6, 7)
TC = SLOTS * D
CH = 25
NP = N // CH
GROUP = 4
GROUPS = -(-CH // GROUP)
ZERO = BATCHES * ROWS
G_UNITS = -(-TB // 2)
EH_GROUPS = ((0, 4), (4, 7), (7, 10), (10, 13))
LN_EPS = 1e-5
assert BATCHES * TB == TILES and ITERS * 2 == BATCHES and sum(HALF) == TB and NP * CH == N


def group_chunks(g):
    return range(g * GROUP, min(CH, g * GROUP + GROUP))


def chunks(g):
    return slice(g * GROUP, min(CH, g * GROUP + GROUP))


def build(nc, x, src_t, dst_t, next_t, ends, attr_t, w1, w2, b2, w_gru, w_lin, conv_b, fold, out):
    with ExitStack() as ctx:
        def sb(name, shape, dt=F32):
            return ctx.enter_context(nc.sbuf_tensor(name, shape, dt))

        def bank(name):
            return ctx.enter_context(nc.psum_tensor(name, [P, 512], F32))

        def sem(name):
            return ctx.enter_context(nc.semaphore(name))

        table = nc.dram_tensor("node_table", (N + 1, D), F32, kind="Internal").ap()
        slot_rows = nc.dram_tensor("slot_rows", (ZERO + 1, D), F32, kind="Internal").ap()

        w1_sb = sb("w1_sb", [P, K])
        w2_sb = sb("w2_sb", [K, D, D])
        b2_sb = sb("b2_sb", [P, D])
        fold_sb = sb("fold_sb", [P, D])
        w_gru_sb = sb("w_gru_sb", [2 * D + 2, 4 * D])
        w_lin_sb = sb("w_lin_sb", [2 * D + 2, D])
        conv_row = sb("conv_row", [1, D])
        conv_sb = sb("conv_sb", [P, D])
        ident = sb("ident", [P, P])
        ones_row = sb("ones_row", [1, P])
        zeros = sb("zeros", [1, D])
        eps = sb("eps", [P, 1])
        src_sb = sb("src_sb", [P, TILES + 2 * TB], I32)
        mask = sb("mask", [P, TILES * SLOTS])
        idx_a = sb("idx_a", [NP, CH], I32)
        idx_b = sb("idx_b", [NP, CH], I32)
        iters_needed = sb("iters_needed", [NP, CH], I32)
        x_sb = sb("x_sb", [NP, CH, D])
        mh = sb("mh", [NP, CH, 2 * D])
        mh_t = sb("mh_t", [2 * D + 2, CH * NP])
        agg_a = sb("agg_a", [NP, CH * D])
        agg_b = sb("agg_b", [NP, CH * D])
        gates = sb("gates", [NP, CH, 2 * D])
        cand = sb("cand", [NP, CH, D])
        cand2 = sb("cand2", [NP, CH, D])
        idx_now = [sb(f"idx_now{u}", [P, TB], I32) for u in range(2)]
        xg = [sb(f"xg{u}", [P, TB * D]) for u in range(2)]
        mask_now = [sb(f"mask_now{u}", [P, TB, SLOTS]) for u in range(2)]
        xm = [sb(f"xm{u}", [P, TB, D, SLOTS]) for u in range(2)]
        attr = [sb(f"attr{u}", [P, TB * P]) for u in range(2)]
        eh = [sb(f"eh{u}", [P, TB * K]) for u in range(2)]
        g_sb = sb("g_sb", [K, D, 2 * TB, SLOTS])
        xs_t = sb("xs_t", [P, ROWS2])
        sum_t = sb("sum_t", [P, ROWS2])
        slot_sb = sb("slot_sb", [ROWS, 2, D])

        eh_ps = [bank(f"eh_ps{i}") for i in range(2)]
        g_ps = [bank(f"g_ps{i}") for i in range(4)]
        sum_ps = bank("sum_ps")
        slot_bank = bank("slot_bank")
        xs_ps = sum_ps[0:D, 256:256 + ROWS2]
        slot_ps = slot_bank[0:ROWS, 0:2 * D]

        x_in = sem("x_in")
        edges_in = sem("edges_in")
        src_in = sem("src_in")
        weights_in = sem("weights_in")
        zero_rows = sem("zero_rows")
        consts = sem("consts")
        consts_dve = sem("consts_dve")
        dve_order = sem("dve_order")
        ends_ps = sem("ends_ps")
        std_ready = sem("std_ready")
        mask_ready = sem("mask_ready")
        node_idx = sem("node_idx")
        idx_staged = sem("idx_staged")
        gathered = [[sem(f"gathered{u}{h}") for h in range(2)] for u in range(2)]
        mask_staged = sem("mask_staged")
        xm_ready = sem("xm_ready")
        attr_zero = sem("attr_zero")
        attr_in = [sem(f"attr_in{u}") for u in range(2)]
        eh_made = sem("eh_made")
        eh_ready = sem("eh_ready")
        g_made = sem("g_made")
        xs_made = sem("xs_made")
        g_act = sem("g_act")
        g_dve = sem("g_dve")
        xs_ready = sem("xs_ready")
        sum_made = sem("sum_made")
        sum_ready = sem("sum_ready")
        slot_made = sem("slot_made")
        slot_copied = sem("slot_copied")
        slot_out = sem("slot_out")
        slot_zero = sem("slot_zero")
        agg_in = [sem(f"agg_in{g}") for g in range(GROUPS)]
        m_ready = sem("m_ready")
        mh_made = sem("mh_made")
        mht_ready = sem("mht_ready")
        gates_made = sem("gates_made")
        rz_ready = sem("rz_ready")
        pre_ready = sem("pre_ready")
        n_ready = sem("n_ready")
        h_ready = sem("h_ready")
        table_out = sem("table_out")
        y_ready = sem("y_ready")
        out_done = sem("out_done")
        pool_passed = sem("pool_passed")
        pe_passed = sem("pe_passed")

        pre = g_sb[:, :, :, :].rearrange("p i t r -> p (i t r)")
        dst_f, nxt_f, first_b, last_b, tile_id, junk = (pre[:, i * TILES:(i + 1) * TILES] for i in range(6))
        dst_i = sb("dst_i", [P, TILES], I32)
        nxt_i = sb("nxt_i", [P, TILES], I32)
        ends_i = sb("ends_i", [1, 2 * TILES], I32)
        ends_f = sb("ends_f", [1, 2 * TILES])
        tid_i = sb("tid_i", [P, TILES], I32)
        node_i = sb("node_i", [NP, CH], I32)
        node_f = sb("node_f", [NP, CH])
        tile_a = sb("tile_a", [NP, CH])
        tile_b = sb("tile_b", [NP, CH])
        first_a = sb("first_a", [NP, CH])
        t0 = sb("t0", [NP, CH])
        t1 = sb("t1", [NP, CH])
        stat = sb("stat", [NP, CH])
        stat2 = sb("stat2", [NP, CH])
        iters_f = sb("iters_f", [NP, CH])

        block = ctx.enter_context(nc.Block())

        @block.sync
        def _(sp):
            sp.dma_start(x_sb[:, :, :], x.rearrange("(c p) d -> p c d", p=NP)).then_inc(x_in, 16)
            sp.dma_start(src_sb[:, :], src_t).then_inc(src_in, 16)
            sp.dma_start(w_lin_sb[:, :], w_lin).then_inc(weights_in, 16)
            sp.dma_start(w1_sb[:, :], w1).then_inc(weights_in, 16)
            sp.dma_start(w2_sb[:, :, :], w2).then_inc(weights_in, 16)
            sp.dma_start(b2_sb[:, :], b2).then_inc(weights_in, 16)
            sp.dma_start(w_gru_sb[:, :], w_gru).then_inc(weights_in, 16)
            sp.dma_start(conv_row[:, :], conv_b).then_inc(weights_in, 16)
            sp.dma_start(fold_sb[:, :], fold).then_inc(weights_in, 16)
            sp.dma_start(ends_i[:, :], ends).then_inc(edges_in, 16)
            sp.dma_start(dst_i[:, :], dst_t).then_inc(edges_in, 16)
            sp.dma_start(nxt_i[:, :], next_t).then_inc(edges_in, 16)
            sp.wait_ge(slot_zero, 1)
            sp.wait_ge(attr_zero, 2)
            sp.dma_start(attr[0][0:D + 1, :], attr_t[:, 0:TB * P]).then_inc(attr_in[0], 16)
            sp.wait_ge(consts, 1)
            sp.dma_start(table[N:N + 1, :], zeros[0:1, :]).then_inc(table_out, 16)
            node_rows = table[0:N, :].rearrange("(c p) d -> p c d", p=NP)
            for g in range(GROUPS):
                sp.wait_ge(h_ready, g + 1)
                sp.dma_start(node_rows[:, chunks(g), :], mh[:, chunks(g), D:2 * D]).then_inc(table_out, 16)
            with sp.Fori(0, STEPS) as s:
                with sp.Fori(0, ITERS) as j:
                    for u in range(2):
                        n = s * BATCHES + j * 2 + u
                        sp.wait_ge(eh_made, n * 4 + 4)
                        sp.dma_start(attr[1 - u][0:D + 1, :], attr_t[:, bass.ds((j * 2 + u + 1) * (TB * P), TB * P)])\
                          .then_inc(attr_in[1 - u], 16)
                for g in range(GROUPS):
                    sp.wait_ge(h_ready, (s + 1) * GROUPS + (g + 1))
                    sp.dma_start(node_rows[:, chunks(g), :], mh[:, chunks(g), D:2 * D]).then_inc(table_out, 16)
            sp.wait_ge(y_ready, 1)
            sp.dma_start(out.rearrange("(c p) d -> p c d", p=NP), mh[:, :, 0:D]).then_inc(out_done, 16)
            sp.wait_ge(out_done, 16)
            sp.wait_ge(table_out, 16 * ((STEPS + 1) * GROUPS + 1))
            sp.wait_ge(attr_in[0], 16 * (STEPS * ITERS + 1))
            sp.wait_ge(attr_in[1], 16 * STEPS * ITERS)

        @block.gpsimd
        def _(pool):
            pool.memset(zeros[:, :], 0.0).then_inc(consts, 1)
            pool.memset(ident[:, :], 0.0).then_inc(consts, 1)
            pool.wait_ge(consts, 2)
            pool.affine_select(out=ident[:, :], in_=ident[:, :], compare_op=ALU.not_equal, fill=1.0, base=0,
                               pattern=[[-1, P]], channel_multiplier=1).then_inc(consts, 1)
            pool.iota(node_i[:, :], pattern=[[NP, CH]], base=0, channel_multiplier=1).then_inc(consts, 1)
            pool.iota(tid_i[:, :], pattern=[[1, TILES]], base=0, channel_multiplier=0).then_inc(consts, 1)
            for u in range(2):
                pool.memset(attr[u][:, :], 0.0).then_inc(attr_zero, 1)
            pool.wait_ge(node_idx, 1)
            needed = [pool.value_load(iters_needed[NP - 1:NP, group_chunks(g)[-1]:group_chunks(g)[-1] + 1],
                                      min_val=0, max_val=ITERS) for g in range(GROUPS)]
            with pool.Fori(0, STEPS) as s:
                pool.wait_ge(table_out, s * (16 * GROUPS) + 16 * (GROUPS + 1))
                pool.sem_inc(pool_passed, 1)
                with pool.Fori(0, ITERS) as j:
                    for u in range(2):
                        n = s * BATCHES + j * 2 + u
                        pool.wait_ge(xs_made, n + 1)
                        pool.wait_ge(idx_staged, n + 1)
                        pool.sem_inc(pool_passed, 1)
                        for t in range(TB):
                            pool.indirect_dma_start(
                                xg[u][:, t * D:(t + 1) * D], None, table,
                                bass.IndirectOffsetOnAxis(ap=idx_now[u][:, t:t + 1], axis=0))\
                                .then_inc(gathered[u][int(t >= HALF[0])], 16)
                for g in range(GROUPS):
                    pool.wait_ge(slot_out, (s * ITERS + needed[g]) * 16 + 32)
                    pool.sem_inc(pool_passed, 1)
                    for c in group_chunks(g):
                        for agg, idx in ((agg_a, idx_a), (agg_b, idx_b)):
                            pool.indirect_dma_start(
                                agg[:, c * D:(c + 1) * D], None, slot_rows,
                                bass.IndirectOffsetOnAxis(ap=idx[:, c:c + 1], axis=0)).then_inc(agg_in[g], 16)

        @block.scalar
        def _(act):
            act.wait_ge(consts, 1)
            act.dma_start(slot_rows[ZERO:ZERO + 1, :], zeros[:, :]).then_inc(slot_out, 16)
            act.wait_ge(attr_zero, 2)
            act.dma_start(slot_rows[0:ZERO, :].rearrange("(p a) d -> p (a d)", a=TB * P // D),
                          attr[1][0:ZERO * D // (TB * P), :]).then_inc(slot_out, 16)
            act.wait_ge(slot_out, 32)
            act.sem_inc(slot_zero, 1)

            act.wait_ge(std_ready, 1)
            nc.scalar.activation(stat[:, :], stat2[:, :], ACT.Sqrt, bias=eps[0:NP, :], scale=1.0 / D)\
                .then_inc(std_ready, 1)

            def transposed(g, done):
                act.wait_ge(mh_made, done + g + 1)
                w = len(group_chunks(g)) * NP
                nc.scalar.copy(mh_t[0:2 * D, g * GROUP * NP:g * GROUP * NP + w], g_ps[g % 2][0:2 * D, 0:w])\
                    .then_inc(mht_ready, 1)

            for g in range(GROUPS):
                transposed(g, 0)
                act.wait_ge(gates_made, g + 1)
                k = len(group_chunks(g))
                nc.scalar.activation(mh[:, g * GROUP:g * GROUP + k, D:2 * D],
                                     g_ps[2 + g % 2][0:NP, :].rearrange("p (c f) -> p c f", f=4 * D)[:, 0:k, 0:D],
                                     ACT.Relu).then_inc(h_ready, 1)

            def relu(n, v, groups):
                for a, b in groups:
                    g = EH_GROUPS.index((a, b))
                    act.wait_ge(eh_made, n * 4 + (4 + g + 1))
                    nc.scalar.activation(eh[v][:, a * K:b * K], eh_ps[g % 2][:, 0:(b - a) * K], ACT.Relu)\
                        .then_inc(eh_ready, 1)

            relu(0, 0, EH_GROUPS)
            with act.Fori(0, STEPS) as s:
                with act.Fori(0, ITERS) as j:
                    for u in range(2):
                        n = s * BATCHES + j * 2 + u
                        for q in range(0, G_UNITS, 2):
                            act.wait_ge(g_made, n * G_UNITS + (q + 1))
                            g_copy(nc.scalar.copy, g_sb, g_ps, u, q).then_inc(g_act, 1)
                        if u == 0:
                            relu(n + 1, 1 - u, EH_GROUPS)
                    m = s * ITERS + j
                    relu(n + 1, 0, EH_GROUPS[:2])
                    act.wait_ge(sum_made, m + 1)
                    nc.scalar.copy(sum_t[:, :], sum_ps[:, 0:ROWS2]).then_inc(sum_ready, 1)
                    relu(n + 1, 0, EH_GROUPS[2:])
                    act.wait_ge(slot_made, m + 1)
                    act.wait_ge(slot_out, m * 16 + 32)
                    nc.scalar.copy(slot_sb[:, :, :].rearrange("p u d -> p (u d)"), slot_ps).then_inc(slot_copied, 1)
                    act.wait_ge(slot_copied, m + 1)
                    act.dma_start(slot_rows[bass.ds(j * ROWS2, ROWS2), :].rearrange("(u p) d -> p u d", u=2),
                                  slot_sb[:, :, :]).then_inc(slot_out, 16)
                for g in range(GROUPS):
                    k = len(group_chunks(g))
                    cs = slice(g * GROUP, g * GROUP + k)
                    transposed(g, (s + 1) * GROUPS)
                    act.wait_ge(gates_made, (s + 1) * GROUPS + (g + 1))
                    gp = g_ps[2 + g % 2][0:NP, :].rearrange("p (c f) -> p c f", f=4 * D)
                    nc.scalar.activation(gates[:, cs, :], gp[:, 0:k, 0:2 * D], ACT.Sigmoid).then_inc(rz_ready, 1)
                    act.wait_ge(pre_ready, s * GROUPS + (g + 1))
                    nc.scalar.activation(cand2[:, cs, :], cand[:, cs, :], ACT.Tanh).then_inc(n_ready, 1)
            act.wait_ge(slot_out, 16 * (STEPS * ITERS + 2))

        @block.vector
        def _(dve):
            order = [0]

            def link(ins, base=0):
                order[0] += 1
                ins.then_inc(dve_order, 1)
                dve.wait_ge(dve_order, base + order[0])

            nc.vector.memset(ones_row[:, :], 1.0).then_inc(consts_dve, 1)
            nc.vector.memset(eps[:, :], LN_EPS).then_inc(consts_dve, 1)
            nc.vector.memset(mh_t[2 * D:2 * D + 2, :], 1.0).then_inc(consts_dve, 1)
            nc.vector.memset(xs_t[:, :], 0.0).then_inc(consts_dve, 1)
            link(nc.vector.memset(mh[:, :, :], 0.0))

            def over_d(a):
                return a[:, :].unsqueeze(2).broadcast_to([NP, CH, D])

            dve.wait_ge(x_in, 16)
            link(nc.vector.reduce_sum(t0[:, :], x_sb[:, :, :], AX.X))
            link(nc.vector.tensor_scalar(t0[:, :], t0[:, :], 1.0 / D, None, ALU.mult))
            link(nc.vector.tensor_tensor(cand[:, :, :], x_sb[:, :, :], over_d(t0), ALU.subtract))
            link(nc.vector.tensor_tensor(cand2[:, :, :], cand[:, :, :], cand[:, :, :], ALU.mult))
            nc.vector.reduce_sum(stat2[:, :], cand2[:, :, :], AX.X).then_inc(std_ready, 1)
            dve.wait_ge(std_ready, 2)
            link(nc.vector.reciprocal(t1[:, :], stat[:, :]))
            link(nc.vector.tensor_tensor(cand2[:, :, :], cand[:, :, :], over_d(t1), ALU.mult))
            nc.vector.tensor_scalar_max(mh[:, :, 0:D], cand2[:, :, :], 0.0).then_inc(m_ready, GROUPS)

            dve.wait_ge(edges_in, 48)
            link(nc.vector.tensor_copy(ends_f[:, :], ends_i[:, :]))
            nc.vector.tensor_copy(dst_f, dst_i[:, :])
            nc.vector.tensor_copy(nxt_f, nxt_i[:, :])
            dve.wait_ge(ends_ps, 1)
            nc.vector.tensor_copy(first_b[:, 0:TILES // 2], g_ps[0][:, 0:TILES // 2])
            nc.vector.tensor_copy(first_b[:, TILES // 2:TILES], g_ps[1][:, 0:TILES // 2])
            nc.vector.tensor_copy(last_b[:, 0:TILES // 2], g_ps[2][:, 0:TILES // 2])
            nc.vector.tensor_copy(last_b[:, TILES // 2:TILES], g_ps[3][:, 0:TILES // 2])
            link(nc.vector.tensor_copy(conv_sb[:, :], sum_ps[:, 0:D]))
            link(nc.vector.tensor_tensor(dst_f, dst_f, first_b, ALU.subtract))
            mask_tr = mask[:, :].rearrange("p (t r) -> p t r", r=SLOTS)
            for r in range(SLOTS):
                nc.vector.tensor_single_scalar(mask_tr[:, :, r], dst_f, float(r), ALU.is_equal)\
                    .then_inc(mask_ready, 1)
            dve.wait_ge(mask_ready, SLOTS)

            dve.wait_ge(consts, 5)
            nc.vector.tensor_copy(tile_id, tid_i[:, :])
            link(nc.vector.tensor_copy(node_f[:, :], node_i[:, :]))
            for c in range(CH):
                node = node_f[:, c:c + 1]
                link(nc.vector.tensor_scalar(junk[0:NP, :], last_b[0:NP, :], node, 0.0, ALU.is_lt, ALU.add,
                                             accum_out=tile_a[:, c:c + 1]))
                link(nc.vector.tensor_scalar(junk[0:NP, :], first_b[0:NP, :], node, 0.0, ALU.is_le, ALU.add,
                                             accum_out=tile_b[:, c:c + 1]))
                link(nc.vector.tensor_scalar(junk[0:NP, 0:ITERS], first_b[0:NP, 0:TILES:2 * TB], node, 0.0, ALU.is_le,
                                             ALU.add, accum_out=iters_f[:, c:c + 1]))
                link(nc.vector.scalar_tensor_tensor(junk[0:NP, :], tile_id[0:NP, :], tile_a[:, c:c + 1],
                                                    first_b[0:NP, :], ALU.is_equal, ALU.mult,
                                                    accum_out=first_a[:, c:c + 1]))
            nc.vector.tensor_copy(iters_needed[:, :], iters_f[:, :])
            link(nc.vector.tensor_scalar(tile_b[:, :], tile_b[:, :], -1.0, None, ALU.add))
            link(nc.vector.tensor_tensor(t0[:, :], tile_b[:, :], tile_a[:, :], ALU.subtract))
            link(nc.vector.tensor_tensor(t1[:, :], node_f[:, :], first_a[:, :], ALU.subtract))
            link(nc.vector.scalar_tensor_tensor(t1[:, :], tile_a[:, :], float(SLOTS), t1[:, :], ALU.mult, ALU.add))
            link(nc.vector.tensor_scalar(t1[:, :], t1[:, :], float(-ZERO), None, ALU.add))
            link(nc.vector.scalar_tensor_tensor(t1[:, :], t0[:, :], 0.0, t1[:, :], ALU.is_ge, ALU.mult))
            link(nc.vector.tensor_scalar(t1[:, :], t1[:, :], float(ZERO), 0.0, ALU.add, ALU.max))
            link(nc.vector.tensor_scalar(t1[:, :], t1[:, :], float(ZERO), None, ALU.min))
            link(nc.vector.tensor_copy(idx_a[:, :], t1[:, :]))
            link(nc.vector.tensor_scalar(t1[:, :], tile_b[:, :], float(SLOTS), float(-ZERO), ALU.mult, ALU.add))
            link(nc.vector.scalar_tensor_tensor(t1[:, :], t0[:, :], 1.0, t1[:, :], ALU.is_equal, ALU.mult))
            link(nc.vector.tensor_scalar(t1[:, :], t1[:, :], float(ZERO), None, ALU.add))
            nc.vector.tensor_copy(idx_b[:, :], t1[:, :]).then_inc(node_idx, 1)

            dve.wait_ge(src_in, 16)
            for u in range(2):
                nc.vector.tensor_copy(idx_now[u][:, :], src_sb[:, u * TB:(u + 1) * TB]).then_inc(idx_staged, 1)
            before = order[0]
            per_step = 5 * GROUPS
            with dve.Fori(0, STEPS) as s:
                with dve.Fori(0, ITERS) as j:
                    for u in range(2):
                        n = s * BATCHES + j * 2 + u
                        dve.wait_ge(xs_made, n + 1)
                        nc.vector.tensor_copy(mask_now[u][:, :, :].rearrange("p t r -> p (t r)"),
                                              mask[:, bass.ds((j * 2 + u) * ROWS, ROWS)]).then_inc(mask_staged, 1)
                        dve.wait_ge(mask_staged, n + 1)
                        t = 0
                        for h in range(2):
                            k = HALF[h]
                            dve.wait_ge(gathered[u][h], (s * ITERS + j) * (16 * k) + 16 * k)
                            xv = xg[u][:, t * D:(t + k) * D].rearrange("p (t i) -> p t i", i=D)
                            nc.vector.tensor_tensor(
                                xm[u][:, t:t + k, :, :], xv.unsqueeze(3).broadcast_to([P, k, D, SLOTS]),
                                mask_now[u][:, t:t + k, :].unsqueeze(2).broadcast_to([P, k, D, SLOTS]),
                                ALU.mult).then_inc(xm_ready, 1)
                            t += k
                        nc.vector.tensor_copy(idx_now[u][:, :], src_sb[:, bass.ds((j * 2 + u + 2) * TB, TB)])\
                            .then_inc(idx_staged, 1)
                        for q in range(1, G_UNITS, 2):
                            dve.wait_ge(g_made, n * G_UNITS + (q + 1))
                            g_copy(nc.vector.tensor_copy, g_sb, g_ps, u, q).then_inc(g_dve, 1)
                        dve.wait_ge(xs_made, n + 3)
                        nc.vector.tensor_copy(xs_t[0:D, u * ROWS:(u + 1) * ROWS], xs_ps[:, u * ROWS:(u + 1) * ROWS]).then_inc(xs_ready, 1)
                base = s * per_step
                for g in range(GROUPS):
                    k = len(group_chunks(g))
                    cs = slice(g * GROUP, g * GROUP + k)
                    fs = slice(g * GROUP * D, (g * GROUP + k) * D)
                    dve.wait_ge(agg_in[g], s * (32 * k) + 32 * k)
                    link(nc.vector.tensor_tensor(agg_a[:, fs], agg_a[:, fs], agg_b[:, fs], ALU.add), base)
                    a3 = agg_a[:, fs].rearrange("p (c d) -> p c d", d=D)
                    link(nc.vector.tensor_tensor(a3, a3, conv_sb[0:NP, :].unsqueeze(1).broadcast_to([NP, k, D]),
                                                 ALU.add), base)
                    nc.vector.tensor_scalar_max(mh[:, cs, 0:D], a3, 0.0).then_inc(m_ready, 1)
                    dve.wait_ge(rz_ready, s * GROUPS + (g + 1))
                    gp = g_ps[2 + g % 2][0:NP, :].rearrange("p (c f) -> p c f", f=4 * D)
                    link(nc.vector.tensor_tensor(cand[:, cs, :], gates[:, cs, 0:D], gp[:, 0:k, 3 * D:4 * D],
                                                 ALU.mult), base)
                    nc.vector.tensor_tensor(cand[:, cs, :], cand[:, cs, :], gp[:, 0:k, 2 * D:3 * D],
                                            ALU.add).then_inc(pre_ready, 1)
                    dve.wait_ge(n_ready, s * GROUPS + (g + 1))
                    link(nc.vector.tensor_tensor(cand[:, cs, :], mh[:, cs, D:2 * D], cand2[:, cs, :],
                                                 ALU.subtract), base)
                    link(nc.vector.tensor_tensor(cand[:, cs, :], cand[:, cs, :], gates[:, cs, D:2 * D],
                                                 ALU.mult), base)
                    nc.vector.tensor_tensor(mh[:, cs, D:2 * D], cand[:, cs, :], cand2[:, cs, :],
                                            ALU.add).then_inc(h_ready, 1)
                assert order[0] == before + per_step
            dve.wait_ge(h_ready, (STEPS + 1) * GROUPS)
            nc.vector.tensor_tensor(mh[:, :, 0:D], x_sb[:, :, :], mh[:, :, D:2 * D], ALU.add).then_inc(y_ready, 1)

        @block.tensor
        def _(pe):
            pe.sem_inc(xs_made, 2)
            pe.sem_inc(eh_made, 4)

            def node_products(g, done, w_sb, m_done):
                pe.wait_ge(m_ready, m_done)
                pe.sem_inc(pe_passed, 1)
                for i, c in enumerate(group_chunks(g)):
                    last = nc.tensor.transpose(g_ps[g % 2][0:2 * D, i * NP:(i + 1) * NP], mh[:, c, :],
                                               ident[0:NP, 0:NP])
                last.then_inc(mh_made, 1)
                pe.wait_ge(mht_ready, done + g + 1)
                for i, c in enumerate(group_chunks(g)):
                    last = nc.tensor.matmul(g_ps[2 + g % 2][0:NP, i * 4 * D:i * 4 * D + w_sb.shape[1]],
                                            mh_t[:, c * NP:(c + 1) * NP], w_sb[:, :], start=True, stop=True)
                last.then_inc(gates_made, 1)

            pe.wait_ge(consts, 3)
            pe.wait_ge(consts_dve, 4)
            pe.wait_ge(weights_in, 112)
            for g in range(GROUPS):
                if g >= 2:
                    pe.wait_ge(h_ready, g - 1)
                node_products(g, 0, w_lin_sb, GROUPS)

            pe.wait_ge(h_ready, GROUPS)
            pe.wait_ge(dve_order, 8 + 0)
            for i in range(4):
                nc.tensor.matmul(g_ps[i][:, 0:TILES // 2], ones_row[:, :],
                                 ends_f[:, i * (TILES // 2):(i + 1) * (TILES // 2)], start=True, stop=True)
            nc.tensor.matmul(sum_ps[:, 0:D], ones_row[:, :], conv_row[:, :], start=True, stop=True)\
                .then_inc(ends_ps, 1)

            def edge_network(n, v, uses, groups):
                pe.wait_ge(attr_in[v], uses)
                for a, b in groups:
                    g = EH_GROUPS.index((a, b))
                    if g >= 2:
                        pe.wait_ge(eh_ready, n * 4 + (g - 1))
                    for t in range(a, b):
                        last = nc.tensor.matmul(eh_ps[g % 2][:, (t - a) * K:(t - a + 1) * K],
                                                attr[v][:, t * P:(t + 1) * P], w1_sb[:, :], start=True, stop=True)
                    last.then_inc(eh_made, 1)

            edge_network(0, 0, 16, EH_GROUPS)
            with pe.Fori(0, STEPS) as s:
                with pe.Fori(0, ITERS) as j:
                    for u in range(2):
                        n = s * BATCHES + j * 2 + u
                        pe.wait_ge(eh_ready, n * 4 + 4)
                        for q in range(G_UNITS):
                            if q == 0:
                                pe.wait_ge(xm_ready, n * 2 + 1)
                            if 2 * q == HALF[0]:
                                pe.wait_ge(xm_ready, n * 2 + 2)
                                if u == 1:
                                    pe.wait_ge(xs_ready, n)
                                for t in range(TB):
                                    last = nc.tensor.matmul(xs_ps[:, u * ROWS + t * SLOTS:u * ROWS + (t + 1) * SLOTS],
                                                            xg[u][:, t * D:(t + 1) * D], mask_now[u][:, t, :],
                                                            start=True, stop=True)
                                last.then_inc(xs_made, 1)
                            if q >= 4:
                                if q % 2:
                                    pe.wait_ge(g_dve, n * 3 + (q - 4 + 1) // 2)
                                else:
                                    pe.wait_ge(g_act, n * 4 + ((q - 4) // 2 + 1))
                            elif u == 1:
                                pe.wait_ge(g_dve if q % 2 else g_act, n * (3 if q % 2 else 4))
                            for t in range(2 * q, min(2 * q + 2, TB)):
                                last = nc.tensor.matmul(
                                    g_ps[q % 4][:, (t % 2) * TC:(t % 2 + 1) * TC], eh[u][:, t * K:(t + 1) * K],
                                    xm[u][:, t, :, :].rearrange("p i r -> p (i r)"), start=True, stop=True)
                            last.then_inc(g_made, 1)
                        if u == 0:
                            edge_network(n + 1, 1, (s * ITERS + j) * 16 + 16, EH_GROUPS)
                    m = s * ITERS + j
                    edge_network(n + 1, 0, m * 16 + 32, EH_GROUPS[:2])
                    pe.wait_ge(g_act, n * 4 + 4)
                    pe.wait_ge(g_dve, n * 3 + 3)
                    pe.wait_ge(xs_ready, n + 1)
                    for i in range(D):
                        q = i % 4
                        nc.tensor.matmul(sum_ps[q * D:(q + 1) * D, 0:ROWS2], w2_sb[:, i, :],
                                         g_sb[:, i, :, :].rearrange("k t r -> k (t r)"),
                                         start=(i < 4), stop=(i >= D - 4 and q > 0), tile_position=(0, q * D))
                    nc.tensor.matmul(sum_ps[0:D, 0:ROWS2], b2_sb[:, :], xs_t[:, :], start=False, stop=True,
                                     tile_position=(0, 0)).then_inc(sum_made, 1)
                    edge_network(n + 1, 0, m * 16 + 32, EH_GROUPS[2:])
                    pe.wait_ge(sum_ready, m + 1)
                    for u in range(2):
                        last = nc.tensor.matmul(slot_ps[:, u * D:(u + 1) * D], sum_t[:, u * ROWS:(u + 1) * ROWS],
                                                fold_sb[:, :], start=True, stop=True)
                    last.then_inc(slot_made, 1)
                for g in range(GROUPS):
                    if g >= 2:
                        pe.wait_ge(pre_ready, s * GROUPS + (g - 1))
                    node_products(g, (s + 1) * GROUPS, w_gru_sb, (s + 1) * GROUPS + (g + 1))


def g_copy(copy, g_sb, g_ps, u, q):
    k = min(2, TB - 2 * q)
    t = u * TB + 2 * q
    return copy(g_sb[:, :, t:t + k, :], g_ps[q % 4][:, 0:k * TC].rearrange("k (t i r) -> k i t r", i=D, r=SLOTS))


def kernel(x, src, dst, edge_attr_32, L0_gnn_lin0_w, L0_gnn_lin0_b, L0_gnn_en1_w, L0_gnn_en1_b, L0_gnn_en2_w,
           L0_gnn_en2_b, L0_gnn_conv_bias, L0_gnn_gru_wih, L0_gnn_gru_whh, L0_gnn_gru_bih, L0_gnn_gru_bhh):
    import concourse.bacc as bacc
    from concourse.bass_utils import run_bass_kernel_spmd

    pad = TILES * P - E
    x, src, dst, attr, w_lin, b_lin, w1, b1, w2, b2, conv_b, wih, whh, bih, bhh = (
        np.asarray(a) for a in (x, src, dst, edge_attr_32, L0_gnn_lin0_w, L0_gnn_lin0_b, L0_gnn_en1_w, L0_gnn_en1_b,
                                L0_gnn_en2_w, L0_gnn_en2_b, L0_gnn_conv_bias, L0_gnn_gru_wih, L0_gnn_gru_whh,
                                L0_gnn_gru_bih, L0_gnn_gru_bhh))

    def zeros(*shape):
        return np.zeros(shape, np.float32)

    src_p = np.concatenate([src, np.full(pad, N, np.int32)])
    dst_p = np.concatenate([dst, np.repeat(dst[-1:], pad)])
    next_p = np.concatenate([dst_p[1:], dst_p[-1:]])
    ends = np.concatenate([dst_p[0::P], dst_p[P - 1::P]])[None, :]
    attr_t = np.concatenate([attr.T, zeros(D, pad)], 1)
    attr_t = np.concatenate([attr_t, np.ones((1, TILES * P), np.float32)], 0)
    attr_t = np.concatenate([attr_t, attr_t[:, 0:TB * P]], 1)
    w_gru = np.concatenate([
        np.concatenate([wih.T, zeros(D, D)], 1),
        np.concatenate([whh.T[:, 0:2 * D], zeros(D, D), whh.T[:, 2 * D:3 * D]], 1),
        np.concatenate([bih, zeros(D)])[None, :],
        np.concatenate([bhh[0:2 * D], zeros(D), bhh[2 * D:3 * D]])[None, :]], 0)
    w_lin_t = np.concatenate([w_lin.T, zeros(D, D), b_lin[None, :], zeros(1, D)], 0)
    arrays = {
        "x_in": x,
        "src_t": np.concatenate([src_p, src_p[0:2 * TB * P]]).reshape(TILES + 2 * TB, P).T,
        "dst_t": dst_p.reshape(TILES, P).T,
        "next_t": next_p.reshape(TILES, P).T,
        "ends": ends,
        "attr_t": attr_t,
        "w1_t": np.concatenate([w1.T, b1[None, :], zeros(P - D - 1, K)], 0),
        "w2_t": w2.reshape(D, D, K).transpose(2, 0, 1),
        "b2_t": np.concatenate([b2.reshape(D, D), zeros(P - D, D)], 0),
        "w_gru_t": w_gru,
        "w_lin_t": w_lin_t,
        "conv_b": conv_b[None, :],
        "fold": np.tile(np.eye(D, dtype=np.float32), (P // D, 1)),
    }
    arrays = {k: np.ascontiguousarray(v) for k, v in arrays.items()}
    nc = bacc.Bacc("TRN2", target_bir_lowering=False, num_devices=1)
    args = [nc.dram_tensor(k, v.shape, mybir.dt.from_np(v.dtype), kind="ExternalInput").ap()
            for k, v in arrays.items()]
    out = nc.dram_tensor("out", (N, D), F32, kind="ExternalOutput").ap()
    build(nc, *args, out)
    r = run_bass_kernel_spmd(nc, [arrays], core_ids=[0])
    return r.results[0]["out"]
```

```python
from contextlib import ExitStack

import numpy as np

import concourse.bass as bass
from concourse import mybir

F32 = mybir.dt.float32
BF16 = mybir.dt.bfloat16
I32 = mybir.dt.int32
ALU = mybir.AluOpType
ACT = mybir.ActivationFunctionType
AX = mybir.AxisListType

P = 128
N = 3125
E = 103125
D = 32
K = 128
STEPS = 6
LN_EPS = 1e-5

TILES = -(-E // P)
TB = 13
BATCHES = TILES // TB
ITERS = BATCHES // 2
HALF = 6
SLOTS = 7
TC = SLOTS * D
ROWS = TB * SLOTS
ROWS2 = 2 * ROWS
ZERO = BATCHES * ROWS
UNITS = -(-TB // 2)
G_BANKS = 3
EH_GROUPS = ((0, 4), (4, 7), (7, 10), (10, 13))

NPE = 4
SKIP = 2
PE_TILES = [(1, t) for t in range(TB - NPE, TB)]
MADE_AHEAD = NPE - 1
READ_AHEAD = NPE - 2

CH = -(-N // P)
NPAD = CH * P
GROUP = 4
GROUPS = -(-CH // GROUP)
LO_CH = 13
SLOT_FILL = ZERO // (TB * P // D) * (TB * P // D)
assert BATCHES * TB == TILES and ITERS * 2 == BATCHES and ITERS > CH


def chunks(g):
    return slice(g * GROUP, min(CH, g * GROUP + GROUP))


def group_size(g):
    return min(CH, g * GROUP + GROUP) - g * GROUP


def fetched(m, w, first):
    return m * (NPE - SKIP) + (w - SKIP + 1) if first else m * NPE - (ITERS * SKIP - w - 1)


def fetches(a, b, first):
    return range(max(a, SKIP if first else 0), b)


def half_tiles(h):
    return slice(0, HALF) if h == 0 else slice(HALF, TB)


def dma_tiles(u, first):
    return [t for t in range(TB) if (u, t) not in PE_TILES[SKIP if first else 0:]]


def dma_count(u, h, first):
    return len([t for t in dma_tiles(u, first) if (t >= HALF) == bool(h)])


def g_bank_wait(u, q):
    if q >= G_BANKS:
        return q - G_BANKS + 1
    if u == 0:
        return None
    return max(p for p in range(UNITS) if p % G_BANKS == q % G_BANKS) - UNITS + 1


def build(nc, x, src_t, src_pe_t, src_pe, dst_rows, dst_t, next_t, attr_t, w1, w2, b2, w_gru, w_lin, conv_b, fold,
          out):
    with ExitStack() as ctx:
        def sb(name, shape, dt=F32):
            return ctx.enter_context(nc.sbuf_tensor(name, shape, dt))

        def bank(name):
            return ctx.enter_context(nc.psum_tensor(name, [P, 512], F32))

        def sem(name):
            return ctx.enter_context(nc.semaphore(name))

        table = nc.dram_tensor("node_table", (NPAD + 1, D), F32, kind="Internal").ap()
        slot_rows = nc.dram_tensor("slot_rows", (ZERO + 1, D), F32, kind="Internal").ap()
        lo_rows = nc.dram_tensor("lo_rows", (ITERS + 1, NPE * P), BF16, kind="Internal").ap()
        eh_rows = nc.dram_tensor("eh_rows", (BATCHES + 1, P, TB * K), F32, kind="Internal").ap()

        node_sums = nc.dram_tensor("node_sums", (NPAD, D), F32, kind="Internal").ap()

        w1_sb = sb("w1_sb", [P, K])
        w2_sb = sb("w2_sb", [K, D, D])
        b2_sb = sb("b2_sb", [P, D])
        fold_sb = sb("fold_sb", [P, D])
        w_gru_sb = sb("w_gru_sb", [2 * D + 2, 4 * D])
        w_lin_sb = sb("w_lin_sb", [2 * D + 2, D])
        conv_row = sb("conv_row", [1, D])
        conv_sb = sb("conv_sb", [P, D])
        ident = sb("ident", [P, P])
        ones_row = sb("ones_row", [1, P])
        zeros = sb("zeros", [1, D])
        eps = sb("eps", [P, 1])
        iota_i = sb("iota_i", [P, TILES], I32)
        iota_f = sb("iota_f", [P, TILES])
        part_i = sb("part_i", [P, 1], I32)
        part_f = sb("part_f", [P, 1])

        src_sb = sb("src_sb", [P, TILES + 2 * TB], I32)
        src_pe_t_sb = sb("src_pe_t_sb", [P, NPE * (ITERS + 1)], I32)
        src_pe_sb = sb("src_pe_sb", [P, NPE * (ITERS + 1)], I32)
        chunk_f = sb("chunk_f", [P, NPE * (ITERS + 1)])
        lo_sb = sb("lo_sb", [P, NPE * (ITERS + 1)], BF16)
        dst_i = sb("dst_i", [P, TILES], I32)
        nxt_i = sb("nxt_i", [P, TILES], I32)
        dst_f = sb("dst_f", [P, TILES])
        junk = sb("junk", [P, TILES])
        first_b = sb("first_b", [P, TILES])
        last_b = sb("last_b", [P, TILES])
        carry_slot = sb("carry_slot", [P, TILES])
        mask = sb("mask", [P, TILES * SLOTS])
        node_i = sb("node_i", [P, CH], I32)
        node_f = sb("node_f", [P, CH])
        tile_a = sb("tile_a", [P, CH])
        tile_b = sb("tile_b", [P, CH])
        first_of_b = sb("first_of_b", [P, CH])
        iters_f = sb("iters_f", [P, CH])
        iters_needed = sb("iters_needed", [P, CH], I32)
        row_idx = sb("row_idx", [P, CH], I32)

        x_sb = sb("x_sb", [P, CH, D])
        mh = sb("mh", [P, CH, 2 * D])
        mh_t = sb("mh_t", [2 * D + 2, CH * P])
        h_parts = sb("h_parts", [P, 3, CH, D], BF16)
        agg = sb("agg", [P, CH, D])
        gates = sb("gates", [P, CH, 2 * D])
        cand = sb("cand", [P, CH, D])
        cand2 = sb("cand2", [P, CH, D])
        t0 = sb("t0", [P, CH])
        t1 = sb("t1", [P, CH])
        var = sb("var", [P, CH])
        std = sb("std", [P, CH])

        unfit = sb("unfit", [P, 1])
        unfit_part = sb("unfit_part", [P, 1])
        unordered = sb("unordered", [P, 4])
        ones_col = sb("ones_col", [P, 1])
        flag = sb("flag", [1, 1], I32)
        b2_row = sb("b2_row", [1, D * D])
        dst_row_i = sb("dst_row_i", [1, P], I32)
        dst_row = sb("dst_row", [1, P])
        dst_col = sb("dst_col", [P, 1])
        same = sb("same", [P, P])
        earlier = sb("earlier", [P, P])
        earlier_n = sb("earlier_n", [P, 1])
        add_f = sb("add_f", [P, 1])
        add_idx = sb("add_idx", [P, 1], I32)
        msg = sb("msg", [P, D])
        msg_sum = sb("msg_sum", [P, D])

        idx_now = [sb(f"idx_now{u}", [P, TB], I32) for u in range(2)]
        xg = [sb(f"xg{u}", [P, TB, D]) for u in range(2)]
        xs_in = [sb(f"xs_in{u}", [P, TB, D]) for u in range(2)]
        mask_now = [sb(f"mask_now{u}", [P, TB, SLOTS]) for u in range(2)]
        xm = [sb(f"xm{u}", [P, TB, D, SLOTS]) for u in range(2)]
        attr = [sb(f"attr{u}", [P, TB * P]) for u in range(2)]
        eh = [sb(f"eh{u}", [P, TB * K]) for u in range(2)]
        g_sb = sb("g_sb", [K, D, 2 * TB, SLOTS])
        xs_t = sb("xs_t", [P, ROWS2])
        sum_t = sb("sum_t", [P, 2 * TB, SLOTS])
        carry_mask = sb("carry_mask", [P, 2 * TB, SLOTS])
        carried = sb("carried", [P, 2 * TB, SLOTS])
        carry = sb("carry", [P, 2 * TB + 1])
        slot_sb = sb("slot_sb", [ROWS, 2, D])
        lo_now = sb("lo_now", [P, NPE * P], BF16)
        pick = sb("pick", [P, NPE * P], BF16)
        chunk_mask = sb("chunk_mask", [P, NPE, CH])
        kept = sb("kept", [P, D, CH])

        eh_ps = [bank(f"eh_ps{i}") for i in range(2)]
        g_ps = [bank(f"g_ps{i}") for i in range(G_BANKS)]
        cand_ps = [bank(f"cand_ps{i}") for i in range(2)]
        slot_bank = bank("slot_bank")
        sum_ps = slot_bank[:, 0:ROWS2]
        xs_ps = slot_bank[0:D, 192:192 + ROWS2]
        slot_ps = slot_bank[0:ROWS, 384:384 + 2 * D]
        spread_ps = [a[:, 0:TILES // 2] for a in (eh_ps[0], eh_ps[1], cand_ps[1], slot_bank)]
        conv_ps = slot_bank[:, 512 - D:512]
        t_ps = g_ps[0:2]
        node_ps = [g_ps[2], cand_ps[0]]

        def cand_banks(first):
            return [cand_ps] if first else [cand_ps, eh_ps]

        x_zero = sem("x_zero")
        x_in = sem("x_in")
        src_in = sem("src_in")
        src_pe_in = sem("src_pe_in")
        edges_in = sem("edges_in")
        edges_next_in = sem("edges_next_in")
        conv_in = sem("conv_in")
        w_lin_in = sem("w_lin_in")
        weights_in = sem("weights_in")
        zeroed = sem("zeroed")
        consts = sem("consts")
        consts_dve = sem("consts_dve")
        dve_order = sem("dve_order")
        prep_order = sem("prep_order")
        order_a = sem("order_a")
        order_b = sem("order_b")
        order_fetch = sem("order_fetch")
        order_c = sem("order_c")
        dst_ready = sem("dst_ready")
        ends_made = sem("ends_made")
        spread_read = sem("spread_read")
        var_ready = sem("var_ready")
        std_ready = sem("std_ready")
        lo_ready = sem("lo_ready")
        lo_out = sem("lo_out")
        lo_in = sem("lo_in")
        pick_ready = sem("pick_ready")
        cand_made = sem("cand_made")
        cand_read = sem("cand_read")
        rows_ready = sem("rows_ready")
        idx_staged = sem("idx_staged")
        gathered = [[sem(f"gathered{u}{h}") for h in range(2)] for u in range(2)]
        xg_read = sem("xg_read")
        xm_ready = sem("xm_ready")
        attr_in = [sem(f"attr_in{u}") for u in range(2)]
        eh_made = sem("eh_made")
        eh_ready = sem("eh_ready")
        eh_out = [sem(f"eh_out{u}") for u in range(2)]
        eh_in = [sem(f"eh_in{u}") for u in range(2)]
        g_made = sem("g_made")
        g_ready = sem("g_ready")
        xs_made = sem("xs_made")
        xs_ready = sem("xs_ready")
        sum_made = sem("sum_made")
        sum_ready = sem("sum_ready")
        sum_carried = sem("sum_carried")
        slot_made = sem("slot_made")
        slot_copied = sem("slot_copied")
        slot_out = sem("slot_out")
        slot_zero = sem("slot_zero")
        agg_in = [sem(f"agg_in{g}") for g in range(GROUPS)]
        m_ready = sem("m_ready")
        mh_made = sem("mh_made")
        mht_ready = sem("mht_ready")
        node_made = sem("node_made")
        rz_ready = sem("rz_ready")
        pre_ready = sem("pre_ready")
        n_ready = sem("n_ready")
        h_ready = sem("h_ready")
        parts_ready = sem("parts_ready")
        table_out = sem("table_out")
        y_ready = sem("y_ready")
        out_done = sem("out_done")
        flag_made = sem("flag_made")
        unfit_ready = sem("unfit_ready")
        flag_ready = sem("flag_ready")
        gp_b2_in = sem("gp_b2_in")
        gp_sums_zero = sem("gp_sums_zero")
        gp_sums_clear = sem("gp_sums_clear")
        gp_order = sem("gp_order")
        gp_free = sem("gp_free")
        gp_idx = sem("gp_idx")
        gp_x = [sem(f"gp_x{odd}") for odd in range(2)]
        gp_attr = [sem(f"gp_attr{odd}") for odd in range(2)]
        gp_dst = [sem(f"gp_dst{odd}") for odd in range(2)]
        gp_eh = sem("gp_eh")
        gp_eh_ready = sem("gp_eh_ready")
        gp_dst_row = sem("gp_dst_row")
        gp_w = sem("gp_w")
        gp_msg = sem("gp_msg")
        gp_sum = sem("gp_sum")
        gp_sum_ready = sem("gp_sum_ready")
        gp_added = [sem(f"gp_added{odd}") for odd in range(2)]
        pool_passed = sem("pool_passed")
        pe_passed = sem("pe_passed")

        full = (N // P) * P
        block = ctx.enter_context(nc.Block())

        def node_io(dram, tile):
            return ((dram[0:full, :].rearrange("(c p) d -> p c d", p=P), tile[:, 0:CH - 1, :]),
                    (dram[full:N, :], tile[0:N - full, CH - 1, :]))

        @block.sync
        def _(sp):
            sp.wait_ge(x_zero, 1)
            for rows, place in node_io(x, x_sb):
                sp.dma_start(place, rows).then_inc(x_in, 16)
            sp.dma_start(dst_i[:, :], dst_t).then_inc(edges_in, 16)
            sp.dma_start(conv_row[:, :], conv_b).then_inc(conv_in, 16)
            sp.dma_start(w_lin_sb[:, :], w_lin).then_inc(w_lin_in, 16)
            sp.dma_start(src_sb[:, :], src_t).then_inc(src_in, 16)
            sp.dma_start(nxt_i[:, :], next_t).then_inc(edges_next_in, 16)
            sp.dma_start(src_pe_t_sb[:, :], src_pe_t).then_inc(src_pe_in, 16)
            sp.dma_start(src_pe_sb[:, :], src_pe.rearrange("a b -> (a b)").rearrange("(p q) -> p q", p=P))\
              .then_inc(src_pe_in, 16)
            for place, rows in ((w1_sb[:, :], w1), (w2_sb[:, :, :], w2), (b2_sb[:, :], b2), (w_gru_sb[:, :], w_gru),
                                (fold_sb[:, :], fold)):
                sp.dma_start(place, rows).then_inc(weights_in, 16)
            sp.wait_ge(zeroed, 3)
            sp.dma_start(table[NPAD:NPAD + 1, :], zeros[:, :]).then_inc(table_out, 16)
            sp.wait_ge(slot_zero, 1)
            sp.dma_start(attr[0][0:D + 1, :], attr_t[:, 0:TB * P]).then_inc(attr_in[0], 16)
            node_rows = table[0:NPAD, :].rearrange("(c p) d -> p c d", p=P)

            def store_features(rounds):
                for g in range(GROUPS):
                    sp.wait_ge(h_ready, rounds * GROUPS + (g + 1))
                    sp.dma_start(node_rows[:, chunks(g), :], mh[:, chunks(g), D:2 * D]).then_inc(table_out, 16)

            store_features(0)
            sp.wait_ge(lo_ready, 1)
            sp.dma_start(lo_rows.rearrange("a b -> (a b)").rearrange("(p q) -> p q", p=P), lo_sb[:, :])\
              .then_inc(lo_out, 16)
            sp.wait_ge(lo_out, 16)
            sp.dma_start(lo_now[:, :], lo_rows[0, :].partition_broadcast(P))\
              .then_inc(lo_in, 16)

            def load_picks(m, j):
                sp.wait_ge(pick_ready, m + 1)
                sp.dma_start(lo_now[:, :], lo_rows[bass.ds(j + 1, 1), :].rearrange("a b -> (a b)")
                             .partition_broadcast(P)).then_inc(lo_in, 16)

            with sp.Fori(0, ITERS) as j:
                for u in range(2):
                    n = j * 2 + u
                    sp.wait_ge(eh_made, n * 4 + 4)
                    sp.dma_start(attr[1 - u][0:D + 1, :], attr_t[:, bass.ds((n + 1) * (TB * P), TB * P)])\
                      .then_inc(attr_in[1 - u], 16)
                    if u == 0:
                        load_picks(j, j)
                    sp.wait_ge(eh_ready, n * 4 + 4)
                    sp.dma_start(eh_rows[bass.ds(n, 1), :, :].rearrange("n p k -> (n p) k"), eh[u][:, :])\
                      .then_inc(eh_out[u], 16)
            sp.wait_ge(eh_ready, BATCHES * 4 + 4)
            sp.dma_start(eh_rows[BATCHES, :, :], eh[0][:, :]).then_inc(eh_out[0], 16)
            sp.wait_ge(eh_out[0], 16 * (ITERS + 1))
            sp.wait_ge(eh_out[1], 16 * (ITERS + 1))
            sp.dma_start(eh[0][:, :], eh_rows[BATCHES, :, :]).then_inc(eh_in[0], 16)
            store_features(1)
            with sp.Fori(1, STEPS) as s:
                with sp.Fori(0, ITERS) as j:
                    for u in range(2):
                        n = s * BATCHES + j * 2 + u
                        sp.wait_ge(g_made, n * UNITS + 2 * UNITS)
                        sp.dma_start(eh[1 - u][:, :], eh_rows[bass.ds(j * 2 + u + 1, 1), :, :]
                                     .rearrange("n p k -> (n p) k")).then_inc(eh_in[1 - u], 16)
                        if u == 0:
                            load_picks(s * ITERS + j, j)
                store_features(s + 1)
            sp.wait_ge(y_ready, 1)
            for rows, place in node_io(out, agg):
                sp.dma_start(rows, place).then_inc(out_done, 16)
            sp.wait_ge(out_done, 32)
            sp.wait_ge(table_out, 16 * ((STEPS + 1) * GROUPS + 1))
            sp.wait_ge(attr_in[0], 16 * (ITERS + 1))
            sp.wait_ge(attr_in[1], 16 * ITERS)
            sp.wait_ge(eh_in[0], 16 * ((STEPS - 1) * ITERS + 1))
            sp.wait_ge(eh_in[1], 16 * (STEPS - 1) * ITERS)
            sp.wait_ge(lo_in, 16 * (STEPS * ITERS + 1))

            sp.wait_ge(flag_ready, 1)
            with sp.If(sp.value_load(flag[0:1, 0:1], min_val=0, max_val=P)):
                sp.dma_start(b2_row[:, :], b2[0:D, :].rearrange("i o -> (i o)").unsqueeze(0)).then_inc(gp_b2_in, 16)
                store_features(STEPS + 1)
                with sp.Fori(0, STEPS) as s:
                    with sp.Fori(0, TILES // 2) as pair:
                        for odd in range(2):
                            t = pair * 2 + odd
                            sp.wait_ge(gp_free, s * TILES + t + 1)
                            sp.dma_start(attr[0][0:D + 1, 0:P], attr_t[:, bass.ds(t * P, P)])\
                              .then_inc(gp_attr[odd], 16)
                            sp.dma_start(dst_row_i[:, :], dst_rows[bass.ds(t, 1), :]).then_inc(gp_dst[odd], 16)
                    store_features(s + (STEPS + 2))
                sp.wait_ge(y_ready, 2)
                for rows, place in node_io(out, agg):
                    sp.dma_start(rows, place).then_inc(out_done, 16)
                sp.wait_ge(out_done, 64)
                sp.wait_ge(table_out, 16 * ((2 * STEPS + 2) * GROUPS + 1))

        @block.gpsimd
        def _(pool):
            pool.memset(x_sb[:, :, :], 0.0).then_inc(x_zero, 1)
            pool.memset(ident[:, :], 0.0).then_inc(consts, 1)
            pool.wait_ge(consts, 1)
            pool.affine_select(out=ident[:, :], in_=ident[:, :], compare_op=ALU.not_equal, fill=1.0, base=0,
                               pattern=[[-1, P]], channel_multiplier=1).then_inc(consts, 1)
            pool.memset(zeros[:, :], 0.0).then_inc(zeroed, 1)
            for u in range(2):
                pool.memset(attr[u][:, :], 0.0).then_inc(zeroed, 1)
            pool.iota(node_i[:, :], pattern=[[P, CH]], base=0, channel_multiplier=1).then_inc(consts, 1)
            pool.iota(iota_i[:, :], pattern=[[1, TILES]], base=0, channel_multiplier=0).then_inc(consts, 1)
            pool.iota(part_i[:, :], pattern=[[0, 1]], base=0, channel_multiplier=1).then_inc(consts, 1)

            def step(s, needed=None):
                pool.wait_ge(table_out, s * (16 * GROUPS) + 16 * (GROUPS + 1))
                pool.sem_inc(pool_passed, 1)
                with pool.Fori(0, ITERS) as j:
                    for u in range(2):
                        n = s * BATCHES + j * 2 + u
                        pool.wait_ge(xg_read, n + 1)
                        pool.wait_ge(idx_staged, n + 1)
                        pool.sem_inc(pool_passed, 1)
                        for t in dma_tiles(u, needed is None):
                            pool.indirect_dma_start(
                                xg[u][:, t, :], None, table,
                                bass.IndirectOffsetOnAxis(ap=idx_now[u][:, t:t + 1], axis=0))\
                                .then_inc(gathered[u][int(t >= HALF)], 16)
                if needed is None:
                    pool.wait_ge(rows_ready, 1)
                    needed = [pool.value_load(iters_needed[P - 1:P, chunks(g).stop - 1:chunks(g).stop],
                                              min_val=0, max_val=ITERS) for g in range(GROUPS)]
                for g in range(GROUPS):
                    pool.wait_ge(slot_out, (s * ITERS + needed[g]) * 16 + 48)
                    pool.sem_inc(pool_passed, 1)
                    for c in range(chunks(g).start, chunks(g).stop):
                        pool.indirect_dma_start(
                            agg[:, c, :], None, slot_rows,
                            bass.IndirectOffsetOnAxis(ap=row_idx[:, c:c + 1], axis=0)).then_inc(agg_in[g], 16)
                return needed

            needed = step(0)
            with pool.Fori(1, STEPS) as s:
                step(s, needed)

            pool.wait_ge(flag_ready, 1)
            with pool.If(pool.value_load(flag[0:1, 0:1], min_val=0, max_val=P)):
                pool.sem_inc(gp_free, 1)
                with pool.Fori(0, STEPS) as s:
                    pool.wait_ge(gp_sums_zero, s + 1)
                    pool.sem_inc(pool_passed, 1)
                    pool.dma_start(node_sums.rearrange("(p a) d -> p (a d)", p=P),
                                   agg[:, :, :].rearrange("p c d -> p (c d)")).then_inc(gp_sums_clear, 16)
                    pool.wait_ge(gp_sums_clear, s * 16 + 16)
                    pool.wait_ge(table_out, s * (16 * GROUPS) + 16 * ((STEPS + 2) * GROUPS + 1))
                    pool.sem_inc(pool_passed, 1)
                    with pool.Fori(0, TILES // 2) as pair:
                        for odd in range(2):
                            c = s * TILES + pair * 2 + odd
                            k = s * (TILES // 2) + pair
                            pool.wait_ge(gp_idx, c + 1)
                            pool.sem_inc(pool_passed, 1)
                            pool.indirect_dma_start(xg[0][:, 0, :], None, table,
                                                    bass.IndirectOffsetOnAxis(ap=idx_now[0][:, 0:1], axis=0))\
                                                        .then_inc(gp_x[odd], 16)
                            pool.wait_ge(gp_sum_ready, c + 1)
                            pool.sem_inc(pool_passed, 1)
                            pool.indirect_dma_start(node_sums, bass.IndirectOffsetOnAxis(ap=add_idx[:, 0:1], axis=0),
                                                    msg_sum[:, :], None, bounds_check=NPAD - 1, oob_is_err=False,
                                                    compute_op=ALU.add).then_inc(gp_added[odd], 16)
                            pool.wait_ge(gp_added[odd], k * 16 + 16)
                            pool.sem_inc(gp_free, 1)
                    node_rows = node_sums.rearrange("(c p) d -> p c d", p=P)
                    for g in range(GROUPS):
                        pool.dma_start(agg[:, chunks(g), :], node_rows[:, chunks(g), :]).then_inc(agg_in[g], 16)

        @block.scalar
        def _(act):
            act.sem_inc(slot_copied, 1)
            act.sem_inc(eh_out[1], 16)
            act.wait_ge(zeroed, 3)
            act.dma_start(slot_rows[ZERO:ZERO + 1, :], zeros[:, :]).then_inc(slot_out, 16)
            act.dma_start(slot_rows[0:SLOT_FILL, :].rearrange("(p a) d -> p (a d)", a=TB * P // D),
                          attr[1][0:SLOT_FILL * D // (TB * P), :]).then_inc(slot_out, 16)
            act.dma_start(slot_rows[SLOT_FILL:ZERO, :].rearrange("r d -> (r d)").unsqueeze(0),
                          attr[1][0:1, 0:(ZERO - SLOT_FILL) * D]).then_inc(slot_out, 16)
            act.wait_ge(slot_out, 48)
            act.sem_inc(slot_zero, 1)

            def first_features(runs):
                act.wait_ge(var_ready, runs + 1)
                nc.scalar.activation(std[:, :], var[:, :], ACT.Sqrt, bias=eps[:, :], scale=1.0 / D)\
                    .then_inc(std_ready, 1)
                rounds = runs * (STEPS + 1)
                for g in range(GROUPS):
                    transposed(g, rounds)
                    act.wait_ge(node_made, rounds * GROUPS + (g + 1))
                    nc.scalar.activation(
                        mh[:, chunks(g), D:2 * D],
                        node_ps[g % 2][:, :].rearrange("p (c f) -> p c f", f=4 * D)[:, 0:group_size(g), 0:D],
                        ACT.Relu).then_inc(h_ready, 1)

            def transposed(g, rounds):
                act.wait_ge(mh_made, rounds * GROUPS + (g + 1))
                w = group_size(g) * P
                nc.scalar.copy(mh_t[0:2 * D, g * GROUP * P:g * GROUP * P + w], t_ps[g % 2][0:2 * D, 0:w])\
                    .then_inc(mht_ready, 1)

            def gates_out(rounds, steps):
                for g in range(GROUPS):
                    transposed(g, rounds)
                    act.wait_ge(node_made, rounds * GROUPS + (g + 1))
                    gp = node_ps[g % 2][:, :].rearrange("p (c f) -> p c f", f=4 * D)
                    nc.scalar.activation(gates[:, chunks(g), :], gp[:, 0:group_size(g), 0:2 * D], ACT.Sigmoid)\
                        .then_inc(rz_ready, 1)
                    act.wait_ge(pre_ready, steps * GROUPS + (g + 1))
                    nc.scalar.activation(cand2[:, chunks(g), :], cand[:, chunks(g), :], ACT.Tanh).then_inc(n_ready, 1)

            first_features(0)

            def relu(n, v, groups, stored=None):
                if 0 in groups and stored is not None:
                    act.wait_ge(eh_out[v], stored)
                for g in groups:
                    a, b = EH_GROUPS[g]
                    act.wait_ge(eh_made, n * 4 + (4 + g + 1))
                    nc.scalar.activation(eh[v][:, a * K:b * K], eh_ps[g % 2][:, 0:(b - a) * K], ACT.Relu)\
                        .then_inc(eh_ready, 1)

            def xs_out(n, u):
                act.wait_ge(xs_made, n + 3)
                nc.scalar.copy(xs_t[0:D, u * ROWS:(u + 1) * ROWS], xs_ps[:, u * ROWS:(u + 1) * ROWS])\
                    .then_inc(xs_ready, 1)

            def g_out(n, u):
                for q in range(UNITS):
                    k = min(2, TB - 2 * q)
                    t = u * TB + 2 * q
                    act.wait_ge(g_made, n * UNITS + (2 * UNITS + q + 1))
                    nc.scalar.copy(g_sb[:, :, t:t + k, :],
                                   g_ps[q % G_BANKS][:, 0:k * TC].rearrange("k (t i r) -> k i t r", i=D, r=SLOTS))\
                        .then_inc(g_ready, 1)
                    if 2 * q == HALF:
                        xs_out(n, u)

            nc.scalar.preload_act_table(ACT.Sigmoid)
            relu(0, 0, range(4))

            def sum_out(m):
                act.wait_ge(sum_made, m + 1)
                nc.scalar.copy(sum_t[:, :, :].rearrange("p t r -> p (t r)"), sum_ps).then_inc(sum_ready, 1)

            def slots_out(m, j):
                act.wait_ge(slot_made, m + 1)
                act.wait_ge(slot_out, m * 16 + 48)
                nc.scalar.copy(slot_sb[:, :, :].rearrange("p u d -> p (u d)"), slot_ps).then_inc(slot_copied, 1)
                act.wait_ge(slot_copied, m + 2)
                act.dma_start(slot_rows[bass.ds(j * ROWS2, ROWS2), :].rearrange("(u p) d -> p u d", u=2),
                              slot_sb[:, :, :]).then_inc(slot_out, 16)

            with act.Fori(0, ITERS) as j:
                n = j * 2
                relu(n + 1, 1, range(4), stored=j * 16 + 16)
                g_out(n, 0)
                relu(n + 2, 0, (0,), stored=j * 16 + 16)
                g_out(n + 1, 1)
                relu(n + 2, 0, (1,))
                sum_out(j)
                relu(n + 2, 0, (2, 3))
                slots_out(j, j)
            gates_out(1, 0)
            with act.Fori(1, STEPS) as s:
                with act.Fori(0, ITERS) as j:
                    n = s * BATCHES + j * 2
                    m = s * ITERS + j
                    g_out(n, 0)
                    g_out(n + 1, 1)
                    sum_out(m)
                    slots_out(m, j)
                gates_out(s + 1, s)
            act.wait_ge(slot_out, 16 * (STEPS * ITERS + 3))

            act.wait_ge(flag_ready, 1)
            with act.If(act.value_load(flag[0:1, 0:1], min_val=0, max_val=P)):
                act.wait_ge(eh_in[0], 16 * ((STEPS - 1) * ITERS + 1))
                first_features(1)
                with act.Fori(0, STEPS) as s:
                    with act.Fori(0, TILES) as t:
                        act.wait_ge(gp_eh, s * TILES + t + 1)
                        nc.scalar.activation(eh[0][:, 0:P], eh_ps[0][:, 0:P], ACT.Relu).then_inc(gp_eh_ready, 1)
                    gates_out(s + (STEPS + 2), s + STEPS)

        @block.vector
        def _(dve):
            def chain(semaphore):
                count = [0]

                def link(ins, base=0):
                    count[0] += 1
                    ins.then_inc(semaphore, 1)
                    dve.wait_ge(semaphore, base + count[0])
                return link, count

            link, links = chain(dve_order)

            nc.vector.memset(ones_row[:, :], 1.0).then_inc(consts_dve, 1)
            nc.vector.memset(eps[:, :], LN_EPS).then_inc(consts_dve, 1)
            nc.vector.memset(ones_col[:, :], 1.0).then_inc(consts_dve, 1)
            nc.vector.memset(mh_t[2 * D:2 * D + 2, :], 1.0).then_inc(consts_dve, 1)
            nc.vector.memset(mh[:, :, D:2 * D], 0.0).then_inc(consts_dve, 1)

            def over_d(a):
                return a[:, :].unsqueeze(2).broadcast_to([P, CH, D])

            def layer_norm(runs):
                if runs > 0:
                    nc.vector.memset(mh[:, :, D:2 * D], 0.0)
                link(nc.vector.reduce_sum(t0[:, :], x_sb[:, :, :], AX.X))
                link(nc.vector.tensor_scalar(t0[:, :], t0[:, :], 1.0 / D, None, ALU.mult))
                link(nc.vector.tensor_tensor(cand[:, :, :], x_sb[:, :, :], over_d(t0), ALU.subtract))
                link(nc.vector.tensor_tensor(cand2[:, :, :], cand[:, :, :], cand[:, :, :], ALU.mult))
                nc.vector.reduce_sum(var[:, :], cand2[:, :, :], AX.X).then_inc(var_ready, 1)
                if runs == 0:
                    dve.wait_ge(edges_in, 16)
                    nc.vector.tensor_copy(dst_f[:, :], dst_i[:, :]).then_inc(dst_ready, 1)
                dve.wait_ge(std_ready, runs + 1)
                link(nc.vector.reciprocal(t1[:, :], std[:, :]))
                link(nc.vector.tensor_tensor(cand2[:, :, :], cand[:, :, :], over_d(t1), ALU.mult))
                nc.vector.tensor_scalar_max(mh[:, :, 0:D], cand2[:, :, :], 0.0).then_inc(m_ready, GROUPS)

            dve.wait_ge(x_in, 32)
            layer_norm(0)

            dve.wait_ge(src_in, 16)
            for u in range(2):
                nc.vector.tensor_copy(idx_now[u][:, :], src_sb[:, u * TB:(u + 1) * TB]).then_inc(idx_staged, 1)
            dve.wait_ge(src_pe_in, 32)
            link(nc.vector.tensor_single_scalar(src_pe_sb[:, :], src_pe_sb[:, :], P - 1, ALU.bitwise_and))
            nc.vector.tensor_copy(lo_sb[:, :], src_pe_sb[:, :]).then_inc(lo_ready, 1)
            link(nc.vector.tensor_single_scalar(src_pe_t_sb[:, :], src_pe_t_sb[:, :], P.bit_length() - 1,
                                                ALU.logical_shift_right))
            link(nc.vector.tensor_copy(chunk_f[:, :], src_pe_t_sb[:, :]))
            dve.wait_ge(consts, 5)
            nc.vector.tensor_copy(iota_f[:, :], iota_i[:, :])
            nc.vector.tensor_copy(part_f[:, :], part_i[:, :])
            nc.vector.tensor_copy(node_f[:, :], node_i[:, :])
            dve.wait_ge(edges_next_in, 16)
            nc.vector.tensor_copy(junk[:, :], nxt_i[:, :])
            nc.vector.memset(xs_t[:, :], 0.0)
            nc.vector.memset(carry[:, 0:1], 0.0)

            dve.wait_ge(ends_made, 1)
            half = TILES // 2
            for place, (row, a) in zip(spread_ps, ((first_b, 0), (first_b, half), (last_b, 0), (last_b, half))):
                nc.vector.tensor_copy(row[:, a:a + half], place)
            link(nc.vector.tensor_copy(conv_sb[:, :], conv_ps))
            dve.sem_inc(spread_read, 1)
            link(nc.vector.tensor_tensor(junk[:, :], dst_f[:, :], junk[:, :], ALU.is_gt))
            link(nc.vector.reduce_max(unfit[:, :], junk[:, :], AX.X))
            link(nc.vector.tensor_tensor(dst_f[:, :], dst_f[:, :], first_b[:, :], ALU.subtract))
            link(nc.vector.reduce_max(unfit_part[:, :], dst_f[:, :], AX.X))
            link(nc.vector.scalar_tensor_tensor(unfit[:, :], unfit_part[:, :], float(SLOTS), unfit[:, :], ALU.is_ge,
                                                ALU.max))
            mask_tr = mask[:, :].rearrange("p (t r) -> p t r", r=SLOTS)
            for r in range(SLOTS):
                nc.vector.tensor_single_scalar(mask_tr[:, :, r], dst_f[:, :], float(r), ALU.is_equal)
            link(nc.vector.memset(carry_slot[:, TILES - 1:TILES], -1.0))
            link(nc.vector.tensor_tensor(junk[:, :], last_b[:, :], first_b[:, :], ALU.subtract))
            link(nc.vector.tensor_scalar(junk[:, :], junk[:, :], 1.0, None, ALU.add))
            link(nc.vector.tensor_tensor(carry_slot[:, 0:TILES - 1], first_b[:, 1:TILES], last_b[:, 0:TILES - 1],
                                         ALU.is_equal))
            link(nc.vector.tensor_tensor(carry_slot[:, 0:TILES - 1], carry_slot[:, 0:TILES - 1],
                                         junk[:, 0:TILES - 1], ALU.mult))
            link(nc.vector.tensor_scalar(carry_slot[:, 0:TILES - 1], carry_slot[:, 0:TILES - 1], -1.0, None, ALU.add))
            link(nc.vector.tensor_scalar(dst_f[:, :], junk[:, :], float(SLOTS), 0.0, ALU.is_gt, ALU.add,
                                         accum_out=unordered[:, 0:1]))
            link(nc.vector.tensor_scalar(dst_f[:, :], junk[:, :], 1.0, 0.0, ALU.is_lt, ALU.add,
                                         accum_out=unordered[:, 1:2]))
            link(nc.vector.tensor_tensor(junk[:, 0:TILES - 1], last_b[:, 0:TILES - 1], first_b[:, 1:TILES], ALU.is_gt))
            link(nc.vector.reduce_max(unordered[:, 2:3], junk[:, 0:TILES - 1], AX.X))

            def split(base=0):
                h = mh[:, :, D:2 * D]
                a, b, c = (h_parts[:, i, :, :] for i in range(3))
                rest = cand[:, :, :]
                link(nc.vector.tensor_copy(a, h), base)
                link(nc.vector.tensor_tensor(rest, h, a, ALU.subtract), base)
                link(nc.vector.tensor_copy(b, rest), base)
                nc.vector.tensor_tensor(c, rest, b, ALU.subtract).then_inc(parts_ready, 1)

            dve.wait_ge(h_ready, GROUPS)
            split()

            link_a, links_a = chain(order_a)
            link_b, links_b = chain(order_b)
            link_c, links_c = chain(order_c)
            per_a, per_b, per_c = 1, 3, 3

            def picks(tiles, m, base):
                dve.wait_ge(lo_in, m * 16 + 16)
                nc.vector.tensor_scalar(pick[:, :], lo_now[:, :], part_f[:, :], None, ALU.is_equal)\
                    .then_inc(pick_ready, 1)
                link_b(nc.vector.tensor_tensor(
                    chunk_mask[:, :, :], iota_f[:, 0:CH].unsqueeze(1).broadcast_to([P, NPE, CH]),
                    chunk_f[:, tiles].unsqueeze(2).broadcast_to([P, NPE, CH]), ALU.is_equal), base)

            picks(slice(0, NPE), 0, 0)

            def wait_gathered(m, u, h, first):
                k = 16 * dma_count(u, h, first)
                before = ITERS * (16 * dma_count(u, h, True) - k)
                dve.wait_ge(gathered[u][h], m * k + k if first else m * k + (k + before))

            def spread(u, h):
                ts = half_tiles(h)
                k = ts.stop - ts.start
                nc.vector.tensor_tensor(
                    xm[u][:, ts, :, :], xg[u][:, ts, :].unsqueeze(3).broadcast_to([P, k, D, SLOTS]),
                    mask_now[u][:, ts, :].unsqueeze(2).broadcast_to([P, k, D, SLOTS]),
                    ALU.mult).then_inc(xm_ready, 1)
                if h == 1:
                    nc.vector.tensor_copy(xs_in[u][:, :, :], xg[u][:, :, :]).then_inc(xg_read, 1)

            def stage_masks(u, j, link, base):
                link(nc.vector.tensor_copy(mask_now[u][:, :, :].rearrange("p t r -> p (t r)"),
                                           mask[:, bass.ds((j * 2 + u) * ROWS, ROWS)]), base)

            def stage_idx(u, j):
                nc.vector.tensor_copy(idx_now[u][:, :], src_sb[:, bass.ds((j * 2 + u + 2) * TB, TB)])\
                    .then_inc(idx_staged, 1)

            def part_a(s, j, half, first):
                m = s * ITERS + j
                if half == 0:
                    dve.wait_ge(g_made, m * (2 * UNITS) + UNITS)
                    links_a[0] = 0
                    stage_masks(0, j, link_a, m * per_a)
                wait_gathered(m, 0, half, first)
                spread(0, half)
                if half == 1:
                    stage_idx(0, j)

            def fetch(m, w, first):
                pairs = cand_banks(first)
                u, t = PE_TILES[w]
                dve.wait_ge(cand_made, fetched(m, w, first))
                for i, cs in enumerate((slice(0, LO_CH), slice(LO_CH, CH))):
                    k = cs.stop - cs.start
                    last = nc.vector.tensor_tensor(
                        kept[:, :, cs], pairs[w % len(pairs)][i][:, 0:k * D].rearrange("p (c i) -> p i c", i=D),
                        chunk_mask[:, w, cs].unsqueeze(1).broadcast_to([P, D, k]), ALU.mult)
                last.then_inc(cand_read, 1)
                dve.wait_ge(cand_read, fetched(m, w, first))
                nc.vector.reduce_sum(xg[u][:, t, :], kept[:, :, :], AX.X).then_inc(order_fetch, 1)
                dve.wait_ge(order_fetch, fetched(m, w, first))

            def part_b(s, j, first):
                m = s * ITERS + j
                n = s * BATCHES + j * 2
                links_b[0] = 1
                base = m * per_b
                stage_masks(1, j, link_b, base)
                link_b(nc.vector.tensor_tensor(
                    carry_mask[:, :, :], iota_f[:, 0:SLOTS].unsqueeze(1).broadcast_to([P, 2 * TB, SLOTS]),
                    carry_slot[:, bass.ds(j * (2 * TB), 2 * TB)].unsqueeze(2).broadcast_to([P, 2 * TB, SLOTS]),
                    ALU.is_equal), base)
                for w in fetches(READ_AHEAD, MADE_AHEAD, first):
                    fetch(m, w, first)
                wait_gathered(m, 1, 0, first)
                spread(1, 0)
                for w in fetches(MADE_AHEAD, NPE, first):
                    fetch(m, w, first)
                wait_gathered(m, 1, 1, first)
                spread(1, 1)
                stage_idx(1, j)
                picks(bass.ds((j + 1) * NPE, NPE), m + 1, base)
                assert links_b[0] - 1 == per_b

            def part_c(s, j):
                m = s * ITERS + j
                links_c[0] = 0
                base = m * per_c
                dve.wait_ge(sum_ready, m + 1)
                link_c(nc.vector.tensor_tensor(carried[:, :, :], sum_t[:, :, :], carry_mask[:, :, :], ALU.mult), base)
                link_c(nc.vector.reduce_sum(carry[:, 1:2 * TB + 1], carried[:, :, :], AX.X), base)
                nc.vector.tensor_tensor(sum_t[:, :, 0], sum_t[:, :, 0], carry[:, 0:2 * TB], ALU.add)\
                    .then_inc(sum_carried, 1)
                dve.wait_ge(sum_carried, m + 1)
                link_c(nc.vector.tensor_copy(carry[:, 0:1], carry[:, 2 * TB:2 * TB + 1]), base)

            def turn(s, j, first):
                m = s * ITERS + j
                part_b(s, j, first)
                part_a(s, j + 1, 0, first)
                for w in fetches(0, READ_AHEAD - 1, first):
                    fetch(m + 1, w, first)
                part_a(s, j + 1, 1, first)
                for w in fetches(READ_AHEAD - 1, READ_AHEAD, first):
                    fetch(m + 1, w, first)
                part_c(s, j)

            def last_turn(s, first):
                part_b(s, ITERS - 1, first)
                part_c(s, ITERS - 1)

            def first_half(s, first):
                for w in fetches(0, READ_AHEAD, first):
                    fetch(s * ITERS, w, first)
                part_a(s, 0, 0, first)
                part_a(s, 0, 1, first)

            def update(rounds, steps, loaded, base, parts=True):
                for g in range(GROUPS + 1):
                    if g < GROUPS:
                        k = group_size(g)
                        dve.wait_ge(agg_in[g], loaded(k))
                        a = agg[:, chunks(g), :]
                        link(nc.vector.tensor_tensor(a, a, conv_sb[:, :].unsqueeze(1).broadcast_to([P, k, D]),
                                                     ALU.add), base)
                        nc.vector.tensor_scalar_max(mh[:, chunks(g), 0:D], a, 0.0).then_inc(m_ready, 1)
                    if g > 0:
                        q = g - 1
                        k = group_size(q)
                        c1, c2 = cand[:, chunks(q), :], cand2[:, chunks(q), :]
                        dve.wait_ge(rz_ready, steps * GROUPS + (q + 1))
                        gp = node_ps[q % 2][:, :].rearrange("p (c f) -> p c f", f=4 * D)
                        link(nc.vector.tensor_tensor(c1, gates[:, chunks(q), 0:D], gp[:, 0:k, 3 * D:4 * D],
                                                     ALU.mult), base)
                        nc.vector.tensor_tensor(c1, c1, gp[:, 0:k, 2 * D:3 * D], ALU.add).then_inc(pre_ready, 1)
                        dve.wait_ge(n_ready, steps * GROUPS + (q + 1))
                        link(nc.vector.tensor_tensor(c1, mh[:, chunks(q), D:2 * D], c2, ALU.subtract), base)
                        link(nc.vector.tensor_tensor(c1, c1, gates[:, chunks(q), D:2 * D], ALU.mult), base)
                        nc.vector.tensor_tensor(mh[:, chunks(q), D:2 * D], c1, c2, ALU.add).then_inc(h_ready, 1)
                if parts:
                    dve.wait_ge(h_ready, rounds * GROUPS + GROUPS)
                    split(base)

            link_p, links_p = chain(prep_order)
            per_chunk = 4

            def find_rows(c):
                one = bass.ds(c, 1)
                node = node_f[:, one]
                links_p[0] = 0
                base = c * per_chunk
                link_p(nc.vector.tensor_scalar(junk[:, :], last_b[:, :], node, 0.0, ALU.is_lt, ALU.add,
                                               accum_out=tile_a[:, one]), base)
                link_p(nc.vector.tensor_scalar(junk[:, 0:ITERS], first_b[:, 0:TILES:2 * TB], node, 0.0, ALU.is_le,
                                               ALU.add, accum_out=iters_f[:, one]), base)
                link_p(nc.vector.tensor_scalar(junk[:, :], first_b[:, :], node, -1.0, ALU.is_le, ALU.add,
                                               accum_out=tile_b[:, one]), base)
                link_p(nc.vector.scalar_tensor_tensor(junk[:, :], iota_f[:, :], tile_b[:, one], first_b[:, :],
                                                      ALU.is_equal, ALU.mult, accum_out=first_of_b[:, one]), base)

            before = links[0]
            first_half(0, True)
            with dve.Fori(0, CH) as j:
                find_rows(j)
                turn(0, j, True)
            with dve.Fori(CH, ITERS - 1) as j:
                turn(0, j, True)
            last_turn(0, True)
            link(nc.vector.reduce_max(unordered[:, 3:4], unordered[:, 0:3], AX.X))
            link(nc.vector.tensor_scalar(unordered[:, 3:4], unordered[:, 3:4], float(ITERS), float(ITERS),
                                         ALU.mult, ALU.min))
            nc.vector.tensor_scalar(iters_needed[:, :], iters_f[:, :], unordered[:, 3:4], None, ALU.max)
            link(nc.vector.tensor_tensor(t0[:, :], tile_b[:, :], tile_a[:, :], ALU.subtract))
            link(nc.vector.reduce_max(unfit_part[:, :], t0[:, :], AX.X))
            nc.vector.scalar_tensor_tensor(unfit[:, :], unfit_part[:, :], 1.0, unfit[:, :], ALU.is_gt,
                                           ALU.max).then_inc(unfit_ready, 1)
            link(nc.vector.tensor_tensor(t1[:, :], node_f[:, :], first_of_b[:, :], ALU.subtract))
            link(nc.vector.scalar_tensor_tensor(t1[:, :], tile_b[:, :], float(SLOTS), t1[:, :], ALU.mult, ALU.add))
            link(nc.vector.tensor_scalar(t1[:, :], t1[:, :], float(-ZERO), None, ALU.add))
            link(nc.vector.scalar_tensor_tensor(t1[:, :], t0[:, :], 0.0, t1[:, :], ALU.is_ge, ALU.mult))
            link(nc.vector.tensor_scalar(t1[:, :], t1[:, :], float(ZERO), 0.0, ALU.add, ALU.max))
            link(nc.vector.tensor_scalar(t1[:, :], t1[:, :], float(ZERO), None, ALU.min))
            nc.vector.tensor_copy(row_idx[:, :], t1[:, :]).then_inc(rows_ready, 1)

            before = links[0]
            per_update = 4 * GROUPS
            update(1, 0, lambda k: 16 * k, 0)
            per_step = links[0] - before
            with dve.Fori(1, STEPS) as s:
                first_half(s, False)
                with dve.Fori(0, ITERS - 1) as j:
                    turn(s, j, False)
                last_turn(s, False)
                links[0] = before
                update(s + 1, s, lambda k: s * (16 * k) + 16 * k, s * per_step)
            links[0] = before + STEPS * per_step

            dve.wait_ge(h_ready, (STEPS + 1) * GROUPS)
            nc.vector.tensor_tensor(agg[:, :, :], x_sb[:, :, :], mh[:, :, D:2 * D], ALU.add).then_inc(y_ready, 1)
            dve.wait_ge(flag_made, 1)
            nc.vector.tensor_copy(flag[:, :], slot_bank[0:1, 0:1]).then_inc(flag_ready, 1)

            dve.wait_ge(flag_ready, 1)
            with dve.If(dve.value_load(flag[0:1, 0:1], min_val=0, max_val=P)):
                dve.wait_ge(out_done, 32)
                layer_norm(1)
                dve.wait_ge(h_ready, (STEPS + 2) * GROUPS)
                before = links[0]
                with dve.Fori(0, STEPS) as s:
                    nc.vector.memset(agg[:, :, :], 0.0).then_inc(gp_sums_zero, 1)
                    with dve.Fori(0, TILES // 2) as pair:
                        for odd in range(2):
                            t = pair * 2 + odd
                            c = s * TILES + t
                            k = s * (TILES // 2) + pair
                            dve.wait_ge(gp_free, c + 1)
                            one = bass.ds(t, 1)
                            nc.vector.tensor_copy(idx_now[0][:, 0:1], src_sb[:, one]).then_inc(gp_idx, 1)
                            dve.wait_ge(gp_dst[odd], k * 16 + 16)
                            nc.vector.tensor_copy(dst_row[:, :], dst_row_i[:, :]).then_inc(gp_dst_row, 1)
                            link_g, links_g = chain(gp_order)
                            per_tile = 8
                            base = c * per_tile
                            link_g(nc.vector.tensor_copy(dst_col[:, :], dst_i[:, one]), base)
                            dve.wait_ge(gp_w, c + 1)
                            dve.wait_ge(gp_x[odd], k * 16 + 16)
                            prod = xm[0][:, :, :, :].rearrange("p t i r -> p (t i r)")[:, 0:D * D]\
                                .rearrange("p (o i) -> p o i", o=D)
                            for q in range(2):
                                i = slice(q * D // 2, (q + 1) * D // 2)
                                ins = nc.vector.tensor_tensor(
                                    prod[:, :, i], cand_ps[q][:, :].rearrange("p (i o) -> p o i", o=D),
                                    xg[0][:, 0, i].unsqueeze(1).broadcast_to([P, D, D // 2]), ALU.mult)
                                if q == 1:
                                    link_g(ins, base)
                            link_g(nc.vector.reduce_sum(msg[:, :], prod, AX.X), base)
                            link_g(nc.vector.tensor_scalar(same[:, :], g_ps[0][:, 0:P], dst_col[:, :], None,
                                                           ALU.is_equal), base)
                            link_g(nc.vector.scalar_tensor_tensor(earlier[:, :], iota_f[:, 0:P], part_f[:, :], same[:, :],
                                                                  ALU.is_lt, ALU.mult), base)
                            link_g(nc.vector.reduce_sum(earlier_n[:, :], earlier[:, :], AX.X), base)
                            link_g(nc.vector.scalar_tensor_tensor(add_f[:, :], earlier_n[:, :], float(NPAD), dst_col[:, :],
                                                                  ALU.mult, ALU.add), base)
                            link_g(nc.vector.tensor_copy(add_idx[:, :], add_f[:, :]), base)
                            assert links_g[0] == per_tile
                            dve.sem_inc(gp_msg, 1)
                            dve.wait_ge(gp_sum, c + 1)
                            nc.vector.tensor_copy(msg_sum[:, :], slot_bank[:, 0:D]).then_inc(gp_sum_ready, 1)
                    links[0] = before
                    update(s + (STEPS + 2), s + STEPS, lambda k: s * 16 + (16 * k * STEPS + 16), s * per_update, False)
                    assert links[0] == before + per_update
                dve.wait_ge(h_ready, (2 * STEPS + 2) * GROUPS)
                nc.vector.tensor_tensor(agg[:, :, :], x_sb[:, :, :], mh[:, :, D:2 * D], ALU.add).then_inc(y_ready, 1)

        @block.tensor
        def _(pe):
            pe.sem_inc(xs_made, 2)
            pe.sem_inc(g_made, 2 * UNITS)
            pe.sem_inc(xg_read, 2)
            pe.sem_inc(eh_made, 4)

            def transposes(g, done, m_done):
                pe.wait_ge(m_ready, m_done)
                if g >= 2:
                    pe.wait_ge(mht_ready, done + (g - 1))
                pe.sem_inc(pe_passed, 1)
                for i in range(group_size(g)):
                    last = nc.tensor.transpose(t_ps[g % 2][0:2 * D, i * P:(i + 1) * P], mh[:, g * GROUP + i, :],
                                               ident[:, :])
                last.then_inc(mh_made, 1)

            def products(g, done, w_sb):
                pe.wait_ge(mht_ready, done + (g + 1))
                for i in range(group_size(g)):
                    c = g * GROUP + i
                    last = nc.tensor.matmul(node_ps[g % 2][:, i * 4 * D:i * 4 * D + w_sb.shape[1]],
                                            mh_t[:, c * P:(c + 1) * P], w_sb[:, :], start=True, stop=True)
                last.then_inc(node_made, 1)

            pe.wait_ge(consts, 2)
            pe.wait_ge(consts_dve, 5)
            pe.wait_ge(conv_in, 16)
            pe.wait_ge(w_lin_in, 16)

            def first_features(runs):
                rounds = runs * (STEPS + 1)
                transposes(0, rounds * GROUPS, (rounds + 1) * GROUPS)
                for g in range(GROUPS):
                    if g + 1 < GROUPS:
                        transposes(g + 1, rounds * GROUPS, (rounds + 1) * GROUPS)
                    if g >= 2:
                        pe.wait_ge(h_ready, rounds * GROUPS + (g - 1))
                    products(g, rounds * GROUPS, w_lin_sb)

            def gate_products(rounds, steps):
                for g in range(GROUPS):
                    transposes(g, rounds * GROUPS, rounds * GROUPS + (g + 1))
                    if g >= 2:
                        pe.wait_ge(pre_ready, steps * GROUPS + (g - 1))
                    products(g, rounds * GROUPS, w_gru_sb)

            pe.wait_ge(dst_ready, 1)
            half = TILES // 2
            for place, (a, b) in zip(spread_ps, ((0, 0), (0, half), (P - 1, 0), (P - 1, half))):
                nc.tensor.matmul(place, ident[:, a:a + 1].broadcast_to([P, P]), dst_f[:, b:b + half],
                                 start=True, stop=True)
            nc.tensor.matmul(conv_ps, ones_row[:, :], conv_row[:, :], start=True, stop=True)\
                .then_inc(ends_made, 1)

            first_features(0)

            def edge_network(n, v, groups, first=False):
                for g in groups:
                    a, b = EH_GROUPS[g]
                    if not (first and g < 2):
                        pe.wait_ge(eh_ready, n * 4 + (g - 1))
                    for t in range(a, b):
                        last = nc.tensor.matmul(eh_ps[g % 2][:, (t - a) * K:(t - a + 1) * K],
                                                attr[v][:, t * P:(t + 1) * P], w1_sb[:, :], start=True, stop=True)
                    last.then_inc(eh_made, 1)

            def fetch(m, w, first):
                pairs = cand_banks(first)
                done = w - (SKIP if first else 0)
                if done == 0:
                    pe.wait_ge(pick_ready, m + 1)
                elif done >= len(pairs):
                    pe.wait_ge(cand_read, fetched(m, w - len(pairs), first))
                for i, cs in enumerate((slice(0, LO_CH), slice(LO_CH, CH))):
                    for part in range(3):
                        last = nc.tensor.matmul(pairs[w % len(pairs)][i][:, 0:(cs.stop - cs.start) * D],
                                                pick[:, w * P:(w + 1) * P],
                                                h_parts[:, part, cs, :].rearrange("p c i -> p (c i)"),
                                                start=(part == 0), stop=(part == 2))
                last.then_inc(cand_made, 1)

            def edge_sums(n, u, loaded=None, between={}):
                if loaded is None:
                    pe.wait_ge(eh_ready, n * 4 + 4)
                else:
                    pe.wait_ge(eh_in[u], loaded)
                for q in range(UNITS):
                    if q == 0:
                        pe.wait_ge(xm_ready, n * 2 + 1)
                    if q in between:
                        fetch(*between[q])
                    if 2 * q == HALF:
                        pe.wait_ge(xm_ready, n * 2 + 2)
                        pe.wait_ge(xg_read, n + 3)
                        if u == 1:
                            pe.wait_ge(xs_ready, n)
                        for t in range(TB):
                            a = u * ROWS + t * SLOTS
                            last = nc.tensor.matmul(xs_ps[:, a:a + SLOTS], xs_in[u][:, t, :], mask_now[u][:, t, :],
                                                    start=True, stop=True)
                        last.then_inc(xs_made, 1)
                    free = g_bank_wait(u, q)
                    if free is not None:
                        pe.wait_ge(g_ready, n * UNITS + free)
                    for t in range(2 * q, min(2 * q + 2, TB)):
                        last = nc.tensor.matmul(g_ps[q % G_BANKS][:, (t % 2) * TC:(t % 2 + 1) * TC],
                                                eh[u][:, t * K:(t + 1) * K],
                                                xm[u][:, t, :, :].rearrange("p i r -> p (i r)"),
                                                start=True, stop=True)
                    last.then_inc(g_made, 1)

            pe.wait_ge(spread_read, 1)
            pe.wait_ge(weights_in, 80)
            pe.wait_ge(attr_in[0], 16)
            edge_network(0, 0, range(4), first=True)

            def slot_sums(n, m):
                pe.wait_ge(g_ready, n * UNITS + 2 * UNITS)
                pe.wait_ge(xs_ready, n + 2)
                for i in range(D):
                    q = i % 4
                    nc.tensor.matmul(sum_ps[q * D:(q + 1) * D, :], w2_sb[:, i, :],
                                     g_sb[:, i, :, :].rearrange("k t r -> k (t r)"),
                                     start=(i < 4), stop=(i >= D - 4 and q > 0), tile_position=(0, q * D))
                nc.tensor.matmul(sum_ps[0:D, :], b2_sb[:, :], xs_t[:, :], start=False, stop=True,
                                 tile_position=(0, 0)).then_inc(sum_made, 1)

            def fold(m):
                pe.wait_ge(sum_carried, m + 1)
                for u in range(2):
                    last = nc.tensor.matmul(slot_ps[:, u * D:(u + 1) * D],
                                            sum_t[:, u * TB:(u + 1) * TB, :].rearrange("p t r -> p (t r)"),
                                            fold_sb[:, :], start=True, stop=True)
                last.then_inc(slot_made, 1)

            def ahead(m, first, units):
                return {units[w]: (m, w, first) for w in fetches(0, min(len(units), READ_AHEAD), first)}

            def first_step_turn(j, more):
                n = j * 2
                pe.wait_ge(attr_in[1], j * 16 + 16)
                edge_network(n + 1, 1, range(4))
                pe.wait_ge(slot_copied, j + 1)
                edge_sums(n, 0, None, {2: (j, NPE - 1, True)})
                pe.wait_ge(attr_in[0], j * 16 + 32)
                edge_network(n + 2, 0, (0,))
                edge_sums(n + 1, 1, None, ahead(j + 1, True, (3, 5)) if more else {})
                edge_network(n + 2, 0, (1,))
                if more:
                    for w in fetches(2, READ_AHEAD, True):
                        fetch(j + 1, w, True)
                slot_sums(n, j)
                edge_network(n + 2, 0, (2, 3))
                if more:
                    for w in fetches(READ_AHEAD, MADE_AHEAD, True):
                        fetch(j + 1, w, True)
                fold(j)

            pe.wait_ge(parts_ready, 1)
            for w in fetches(0, MADE_AHEAD, True):
                fetch(0, w, True)
            with pe.Fori(0, ITERS - 1) as j:
                first_step_turn(j, True)
            first_step_turn(ITERS - 1, False)
            gate_products(1, 0)

            def turn(s, j, more):
                n = s * BATCHES + j * 2
                m = s * ITERS + j
                loaded = (s - 1) * (ITERS * 16) + j * 16 + 16
                pe.wait_ge(slot_copied, m + 1)
                edge_sums(n, 0, loaded, {0: (m, NPE - 1, False)})
                edge_sums(n + 1, 1, loaded, ahead(m + 1, False, (3, 4, 6)) if more else {})
                slot_sums(n, m)
                if more:
                    for w in range(READ_AHEAD, MADE_AHEAD):
                        fetch(m + 1, w, False)
                fold(m)

            with pe.Fori(1, STEPS) as s:
                pe.wait_ge(parts_ready, s + 1)
                pe.sem_inc(pe_passed, 1)
                for w in range(MADE_AHEAD):
                    fetch(s * ITERS, w, False)
                with pe.Fori(0, ITERS - 1) as j:
                    turn(s, j, True)
                turn(s, ITERS - 1, False)
                gate_products(s + 1, s)

            pe.wait_ge(unfit_ready, 1)
            pe.wait_ge(slot_copied, STEPS * ITERS + 1)
            nc.tensor.matmul(slot_bank[0:1, 0:1], unfit[:, :], ones_col[:, :], start=True, stop=True)\
                .then_inc(flag_made, 1)
            pe.wait_ge(flag_ready, 1)
            with pe.If(pe.value_load(flag[0:1, 0:1], min_val=0, max_val=P)):
                first_features(1)
                pe.wait_ge(gp_b2_in, 16)
                with pe.Fori(0, STEPS) as s:
                    with pe.Fori(0, TILES // 2) as pair:
                        for odd in range(2):
                            t = pair * 2 + odd
                            c = s * TILES + t
                            k = s * (TILES // 2) + pair
                            pe.wait_ge(gp_attr[odd], k * 16 + 16)
                            nc.tensor.matmul(eh_ps[0][:, 0:P], w1_sb[:, :], attr[0][:, 0:P], start=True, stop=True)\
                                .then_inc(gp_eh, 1)
                            pe.wait_ge(gp_dst_row, c + 1)
                            nc.tensor.matmul(g_ps[0][:, 0:P], ones_row[:, :], dst_row[:, :], start=True, stop=True)
                            pe.wait_ge(gp_eh_ready, c + 1)
                            w2_cols = w2_sb[:, :, :].rearrange("k i o -> k (i o)")
                            for q in range(2):
                                cols = slice(q * D * D // 2, (q + 1) * D * D // 2)
                                nc.tensor.matmul(cand_ps[q][:, :], eh[0][:, 0:P], w2_cols[:, cols], start=True, stop=False)
                                last = nc.tensor.matmul(cand_ps[q][:, :], ones_row[:, :], b2_row[:, cols],
                                                        start=False, stop=True)
                            last.then_inc(gp_w, 1)
                            pe.wait_ge(gp_msg, c + 1)
                            nc.tensor.matmul(slot_bank[:, 0:D], same[:, :], msg[:, :], start=True, stop=True)\
                                .then_inc(gp_sum, 1)
                    gate_products(s + (STEPS + 2), s + STEPS)


def kernel(x, src, dst, edge_attr_32, L0_gnn_lin0_w, L0_gnn_lin0_b, L0_gnn_en1_w, L0_gnn_en1_b, L0_gnn_en2_w,
           L0_gnn_en2_b, L0_gnn_conv_bias, L0_gnn_gru_wih, L0_gnn_gru_whh, L0_gnn_gru_bih, L0_gnn_gru_bhh):
    import concourse.bacc as bacc
    from concourse.bass_utils import run_bass_kernel_spmd

    pad = TILES * P - E
    x, src, dst, attr, w_lin, b_lin, w1, b1, w2, b2, conv_b, wih, whh, bih, bhh = (
        np.asarray(a) for a in (x, src, dst, edge_attr_32, L0_gnn_lin0_w, L0_gnn_lin0_b, L0_gnn_en1_w, L0_gnn_en1_b,
                                L0_gnn_en2_w, L0_gnn_en2_b, L0_gnn_conv_bias, L0_gnn_gru_wih, L0_gnn_gru_whh,
                                L0_gnn_gru_bih, L0_gnn_gru_bhh))

    def zeros(*shape):
        return np.zeros(shape, np.float32)

    src_p = np.concatenate([src, np.full(pad, NPAD, np.int32)]).reshape(TILES, P)
    dst_p = np.concatenate([dst, np.repeat(dst[-1:], pad)])
    next_p = np.concatenate([dst_p[1:], dst_p[-1:]])
    src_p = np.concatenate([src_p, src_p[0:2 * TB]], 0)
    src_pe = np.stack([src_p[u * TB + t::2 * TB] for u, t in PE_TILES], 1).reshape(ITERS + 1, NPE * P)
    attr_t = np.concatenate([attr.T, zeros(D, pad)], 1)
    attr_t = np.concatenate([attr_t, np.ones((1, TILES * P), np.float32)], 0)
    attr_t = np.concatenate([attr_t, attr_t[:, 0:TB * P]], 1)
    w_gru = np.concatenate([
        np.concatenate([wih.T, zeros(D, D)], 1),
        np.concatenate([whh.T[:, 0:2 * D], zeros(D, D), whh.T[:, 2 * D:3 * D]], 1),
        np.concatenate([bih, zeros(D)])[None, :],
        np.concatenate([bhh[0:2 * D], zeros(D), bhh[2 * D:3 * D]])[None, :]], 0)
    arrays = {
        "x_in": x,
        "src_t": src_p.T,
        "src_pe_t": src_pe.reshape(-1, P).T,
        "src_pe": src_pe,
        "dst_rows": dst_p.reshape(TILES, P),
        "dst_t": dst_p.reshape(TILES, P).T,
        "next_t": next_p.reshape(TILES, P).T,
        "attr_t": attr_t,
        "w1_t": np.concatenate([w1.T, b1[None, :], zeros(P - D - 1, K)], 0),
        "w2_t": w2.reshape(D, D, K).transpose(2, 0, 1),
        "b2_t": np.concatenate([b2.reshape(D, D), zeros(P - D, D)], 0),
        "w_gru_t": w_gru,
        "w_lin_t": np.concatenate([w_lin.T, zeros(D, D), b_lin[None, :], zeros(1, D)], 0),
        "conv_b": conv_b[None, :],
        "fold": np.tile(np.eye(D, dtype=np.float32), (P // D, 1)),
    }
    arrays = {k: np.ascontiguousarray(v) for k, v in arrays.items()}
    nc = bacc.Bacc("TRN2", target_bir_lowering=False, num_devices=1)
    args = [nc.dram_tensor(k, v.shape, mybir.dt.from_np(v.dtype), kind="ExternalInput").ap()
            for k, v in arrays.items()]
    out = nc.dram_tensor("out", (N, D), F32, kind="ExternalOutput").ap()
    build(nc, *args, out)
    r = run_bass_kernel_spmd(nc, [arrays], core_ids=[0])
    return r.results[0]["out"]
```
